# Optimizing a Trainium2 kernel written in Bass

```python
import numpy as np
import jax
import jax.numpy as jnp

def _softmax(x, axis=-1):
    return jax.nn.softmax(x, axis=axis)

def _gelu(x):
    return jax.nn.gelu(x, approximate=True)

def _silu(x):
    return jax.nn.silu(x)

def _sigmoid(x):
    return jax.nn.sigmoid(x)

def _layernorm(x, axis=-1, eps=1e-05):
    m = jnp.mean(x, axis=axis, keepdims=True)
    v = jnp.var(x, axis=axis, keepdims=True)
    return (x - m) / jnp.sqrt(v + eps)

def _scatter_add(tgt, idx, src, axis=0):
    return tgt.at[idx].add(src)

def _segment_sum(src, seg, n):
    return jax.ops.segment_sum(src, seg, n)
kernel_name = 'mk_adaln_d1_jaxref_r8_39fba8'

def setup_inputs(seed: int=0):
    np.random.seed(seed)
    _w = jnp.asarray

    def _L0_attn_setup():
        import jax, jax.numpy as jnp
        import numpy as np
        N_HEADS = 16

        def _alibi_causal_mask(T, n_heads, dtype):
            slopes = (1.0 / jnp.power(2.0, jnp.arange(1, n_heads + 1, dtype=dtype)))[:, None, None]
            idx = jnp.arange(T)
            rel = (idx[None, :] - idx[:, None]).astype(dtype)
            alibi = jnp.tril(rel)
            causal = jnp.where(idx[None, :] > idx[:, None], -jnp.inf, 0.0).astype(dtype)
            return (alibi + causal)[None, :, :] * slopes
        key = jax.random.key(seed)
        ks = jax.random.split(key, 5)
        B, T, C = (2, 256, 128)
        scale = 0.02
        return {'x': jax.random.normal(ks[0], (B, T, C), dtype=jnp.float32), 'W_attn': jax.random.normal(ks[1], (C, 3 * C), dtype=jnp.float32) * scale, 'b_attn': jax.random.normal(ks[2], (3 * C,), dtype=jnp.float32) * scale, 'W_proj': jax.random.normal(ks[3], (C, C), dtype=jnp.float32) * scale, 'b_proj': jax.random.normal(ks[4], (C,), dtype=jnp.float32) * scale}
    _L0_attn_in = _L0_attn_setup()

    def _L0_ffn_setup():
        import jax, jax.numpy as jnp
        import numpy as np
        B, S, D, F_DIM, E, TOPK = (2, 128, 128, 512, 8, 2)
        key = jax.random.key(seed)
        k0, k1, k2, k3 = jax.random.split(key, 4)
        hidden_states = jax.random.normal(k0, (B, S, D), dtype=jnp.float32)
        router_w = jax.random.normal(k1, (E, D), dtype=jnp.float32) * 0.02
        w1 = jax.random.normal(k2, (E, F_DIM, D), dtype=jnp.float32) * 0.02
        w2 = jax.random.normal(k3, (E, D, F_DIM), dtype=jnp.float32) * 0.02
        expert_scale = jnp.ones((E,), dtype=jnp.float32)
        return {'hidden_states': hidden_states, 'router_w': router_w, 'w1': w1, 'w2': w2, 'expert_scale': expert_scale}
    _L0_ffn_in = _L0_ffn_setup()
    _L0_c = _w((lambda *s: np.random.randn(*s).astype(np.float32) * 0.05)(1, 128))
    _L0_wmod = _w((lambda *s: np.random.randn(*s).astype(np.float32) * 0.05)(128, 6 * 128) * 128 ** (-0.5))
    _d = {'L0_attn_x': _L0_attn_in['x'], 'L0_attn_W_attn': _L0_attn_in['W_attn'], 'L0_attn_b_attn': _L0_attn_in['b_attn'], 'L0_attn_W_proj': _L0_attn_in['W_proj'], 'L0_attn_b_proj': _L0_attn_in['b_proj'], 'L0_ffn_router_w': _L0_ffn_in['router_w'], 'L0_ffn_w1': _L0_ffn_in['w1'], 'L0_ffn_w2': _L0_ffn_in['w2'], 'L0_ffn_expert_scale': _L0_ffn_in['expert_scale'], 'L0_c': _L0_c, 'L0_wmod': _L0_wmod}
    _x0 = _d['L0_attn_x']
    _d['L0_attn_x'] = jax.random.normal(jax.random.fold_in(jax.random.key(seed), 1), (1, 2048, 128), dtype=_x0.dtype)
    del _x0
    return _d

def reference(L0_attn_x, L0_attn_W_attn, L0_attn_b_attn, L0_attn_W_proj, L0_attn_b_proj, L0_ffn_router_w, L0_ffn_w1, L0_ffn_w2, L0_ffn_expert_scale, L0_c, L0_wmod):

    def _L0_attn_ref(x, W_attn, b_attn, W_proj, b_proj):
        import jax, jax.numpy as jnp
        import numpy as np
        N_HEADS = 16

        def _alibi_causal_mask(T, n_heads, dtype):
            slopes = (1.0 / jnp.power(2.0, jnp.arange(1, n_heads + 1, dtype=dtype)))[:, None, None]
            idx = jnp.arange(T)
            rel = (idx[None, :] - idx[:, None]).astype(dtype)
            alibi = jnp.tril(rel)
            causal = jnp.where(idx[None, :] > idx[:, None], -jnp.inf, 0.0).astype(dtype)
            return (alibi + causal)[None, :, :] * slopes
        B, T, C = x.shape
        H = N_HEADS
        D = C // H
        qkv = x @ W_attn + b_attn
        q, k, v = jnp.split(qkv, 3, axis=-1)
        q = q.reshape(B, T, H, D).transpose(0, 2, 1, 3)
        k = k.reshape(B, T, H, D).transpose(0, 2, 1, 3)
        v = v.reshape(B, T, H, D).transpose(0, 2, 1, 3)
        att = jnp.einsum('bhtd,bhsd->bhts', q, k) / jnp.sqrt(jnp.asarray(D, x.dtype))
        att = att + _alibi_causal_mask(T, H, x.dtype)[None]
        att = jax.nn.softmax(att, axis=-1)
        y = jnp.einsum('bhts,bhsd->bhtd', att, v)
        y = y.transpose(0, 2, 1, 3).reshape(B, T, C)
        return y @ W_proj + b_proj

    def _L0_ffn_ref(hidden_states, router_w, w1, w2, expert_scale):
        import jax, jax.numpy as jnp
        import numpy as np
        B, S, D, F_DIM, E, TOPK = (2, 128, 128, 512, 8, 2)
        b, s, d = hidden_states.shape
        xf = hidden_states.reshape(-1, d)
        logits = xf @ router_w.T
        probs = jax.nn.softmax(logits, axis=-1)
        top_w, top_idx = jax.lax.top_k(probs, TOPK)
        top_w = jax.nn.softmax(top_w, axis=-1)
        combine = jnp.sum(jax.nn.one_hot(top_idx, E, dtype=xf.dtype) * top_w[..., None], axis=1)
        h = jax.nn.silu(jnp.einsum('td,efd->tef', xf, w1))
        y = jnp.einsum('tef,edf->ted', h, w2)
        y = y * expert_scale[None, :, None]
        out = jnp.einsum('te,ted->td', combine, y)
        return out.reshape(b, s, d)
    x = L0_attn_x
    mod = (_silu(L0_c) @ L0_wmod).reshape(L0_c.shape[0], 6, 1, -1)
    sa, ca, ga, sb, cb, gb = (mod[:, 0], mod[:, 1], mod[:, 2], mod[:, 3], mod[:, 4], mod[:, 5])
    ga = (2 * (ga >= 0) - 1) * jnp.maximum(jnp.abs(ga), 0.25)
    gb = (2 * (gb >= 0) - 1) * jnp.maximum(jnp.abs(gb), 0.25)
    h = _layernorm(x, axis=-1) * (1 + ca) + sa
    x = x + ga * _L0_attn_ref(h, L0_attn_W_attn, L0_attn_b_attn, L0_attn_W_proj, L0_attn_b_proj)
    h = _layernorm(x, axis=-1) * (1 + cb) + sb
    x = x + gb * _L0_ffn_ref(h, L0_ffn_router_w, L0_ffn_w1, L0_ffn_w2, L0_ffn_expert_scale)
    return x

_drawn_inputs = setup_inputs


def setup_inputs(seed=0):
    import zlib

    import numpy as np

    out = dict(_drawn_inputs(seed))
    spreads = {'L0_ffn_expert_scale': (1.0, 0.6)}
    factors = {'L0_attn_W_attn': 8.0,
     'L0_attn_b_attn': 8.0,
     'L0_attn_W_proj': 8.0,
     'L0_attn_b_proj': 8.0,
     'L0_ffn_router_w': 7.208,
     'L0_ffn_w1': 6.346,
     'L0_ffn_w2': 6.311,
     'L0_c': 5.332,
     'L0_wmod': 5.65}
    for name, (base, spread) in spreads.items():
        noise = np.random.default_rng([zlib.crc32(name.encode()), seed]).standard_normal(out[name].shape)
        drawn = base * np.exp(spread * noise) if base else spread * noise
        out[name] = jnp.asarray(drawn.astype(out[name].dtype))
    for name, factor in factors.items():
        out[name] = (out[name] * factor).astype(out[name].dtype)
    return out
```

```python
from contextlib import ExitStack

import numpy as np

import concourse.bass as bass
from concourse import mybir

T, C, H, D = 2048, 128, 16, 8
P = 128
NT = T // P
CW = 512
NC_ = T // CW
TPC = CW // P
HG = 4
G = H // HG
E, F, TOPK = 8, 512, 2
FC = F // P
EPS = 1e-5
BIG = -1e30

PAIR = 3 * D
ALIBI0 = 3 * PAIR
MAX0 = 93
ROWS1, ROWS2 = MAX0, MAX0 + 3
PAD0 = 64

STEPS = [(j, sb) for j in range(NC_) for sb in range(TPC * (j + 1))]
START = [0, 4, 12, 24, 40]
NSTEP = len(STEPS)
TASKS = [(j, c, r, hh) for j in range(NC_) for c in range(j + 1) for r in range(TPC) for hh in range(HG)]
NTASK = len(TASKS)
LEAD = 20
SECTION = 4
RING1, RING2 = 4, 3


KNOTS = {True: [(0, 8), (2, 13), (4, 15), (10, 25), (12, 27), (22, 41), (24, 43), (NSTEP, NSTEP + LEAD)],
         False: [(0, LEAD), (NSTEP, NSTEP + LEAD)]}


def ahead(p, first):
    for (p0, m0), (p1, m1) in zip(KNOTS[first], KNOTS[first][1:]):
        if p <= p1:
            return m0 + (m1 - m0) * (p - p0) // (p1 - p0)


def turns(p, first, last):
    at = {}
    for q in range(NSTEP, -1, -1):
        for u in range(2 * NC_):
            if ahead(q, first) > START[u % NC_ + 1] + NSTEP * (u // NC_):
                at[u] = q
    return [u for u, q in at.items() if p >= -1 and q == max(p, 0) and (p == -1) == (first and u == 0) and q < NSTEP
            and (first or u >= NC_ or q > 0) and not (last and u >= NC_)]


def width(j, sb):
    return CW - P * max(0, sb - TPC * j)


def take(e, s, n):
    e.wait_ge(s, n)
    e.sem_inc(s, -n)


class Own:

    def __init__(self, e, s):
        self.e, self.s, self.n = e, s, 0

    def inc(self, ins):
        self.n += 1
        ins.then_inc(self.s, 1)
        return self.n

    def wait(self, n=None):
        self.e.wait_ge(self.s, self.n if n is None else n)

    def reset(self):
        self.wait()
        self.e.sem_inc(self.s, -self.n)
        self.n = 0


def build(nc, a):
    fp32, bf16 = mybir.dt.float32, mybir.dt.bfloat16
    ALU, ACT, AX = mybir.AluOpType, mybir.ActivationFunctionType, mybir.AxisListType
    ds = bass.ds
    with ExitStack() as ctx:
        def sb(name, shape, dt=fp32):
            return ctx.enter_context(nc.sbuf_tensor(name, shape, dt))

        def sem(name):
            return ctx.enter_context(nc.semaphore(name))

        x_sb = sb("x_sb", [P, NT, C])
        ident = sb("ident_sb", [P, P])
        mask = sb("mask_sb", [P, CW])
        wqkv = sb("wqkv", [P, 3 * C])
        bqk = sb("bqk", [P, 2])
        bv_bc = sb("bv_bc", [P, C])
        wproj = sb("wproj_sb", [P, G, C])
        ccol = sb("ccol", [P, 1])
        wmod = sb("wmod", [P, 6 * C])
        rwT = sb("rwT_sb", [P, E])
        scale_bc = sb("scale_bc", [P, E])
        tri8 = sb("tri8_sb", [P, E, E])
        sil = sb("sil", [P, 1])
        ones = sb("ones", [P, P])
        silbc = sb("silbc", [P, P])
        modc = sb("modc", [P, 4])
        gsgn = sb("gsgn", [P, 2, C])
        gabs = sb("gabs", [P, 2, C])
        gate = sb("gate", [P, 2, C])
        stats = sb("stats", [P, NT, 6])
        mv = sb("mv", [P, NT, 2])
        rstd = sb("rstd", [P, NT])
        std = sb("std", [P, NT])
        xn = sb("xn", [P, NT, C])
        hT = sb("hT", [P, T])
        q32 = sb("q32", [P, 2, CW])
        res = sb("res", [P, 2, CW])
        pieces = sb("pieces", [P, 2, 2, 3, CW], bf16)
        v_all = xn
        v_cur = sb("v_cur", [P, NT, HG, 32])
        q_aug = sb("q_aug", [P, 2 * HG * T], bf16)
        k_aug = sb("k_aug", [P, 2 * HG * T], bf16)
        w1T = q_aug[:, 0:HG * T].bitcast(fp32)
        w2T = k_aug[:, 0:HG * T].bitcast(fp32).rearrange("p (n c) -> p n c", c=C)
        part = sb("part", [P, 2, TPC * HG, NC_])
        junk = sb("junk", [P, RING1, CW], bf16)
        nmax = sb("nmax", [P, 2, TPC, HG])
        nres = sb("nres", [P, 2, TPC, HG])
        nmp = sb("nmp", [P, 2, TPC, 3, HG], bf16)
        identb = sb("identb", [P, P], bf16)
        rows = sb("rows", [3 * HG, 2, CW], bf16)
        tick = sb("tick", [P, 32])
        probs = sb("probs", [P, 2, HG, CW])
        yT = hT[:, 0:2 * CW].rearrange("p (k t) -> p k t", k=2)
        yB = hT[:, 2 * CW:4 * CW].rearrange("p (k b q) -> p k b q", k=2, q=32)
        yN = sb("yN", [P, 2, CW // 32, 32])
        rl = sb("rl", [P, 2, CW // 32])
        yn = sb("yn", [P, G * T])
        lmax = sb("lmax", [P, NT])
        lg = sb("lg", [P, NT, E])
        pr = sb("pr", [P, NT, E])
        psm = sb("psm", [P, NT])
        ptop = sb("ptop", [P, 2, NT])
        gt = q32[:, :, :].rearrange("p k (n e f) -> p (k n) e f", e=E, f=E)
        eq = res[:, :, :].rearrange("p k (n e f) -> p (k n) e f", e=E, f=E)
        rank = sb("rank", [P, NT, E])
        hot = sb("hot", [P, 2, NT, E])
        wtop = sb("wtop", [P, 2, NT])
        comb = sb("comb", [P, NT, E])
        hs = probs
        accO = sb("accO", [P, TPC, C])

        b1 = ctx.enter_context(nc.psum_tensor("b1", [P, RING1, CW], fp32))
        b2 = ctx.enter_context(nc.psum_tensor("b2", [P, RING2, CW], fp32))
        pv = ctx.enter_context(nc.psum_tensor("pv", [P, CW], fp32))

        q_dram = nc.dram_tensor("q_scratch", (3, P, 3, T), bf16, kind="Internal").ap()
        k_dram = nc.dram_tensor("k_scratch", (P, 3, T), bf16, kind="Internal").ap()

        x_in = [sem(f"x_in{c}") for c in range(NC_)]
        small_in, late_in = sem("small_in"), sem("late_in")
        pad_set, pads_set = sem("pad_set"), sem("pads_set")
        dve_s, act_s, pool_s = sem("dve_self"), sem("act_self"), sem("pool_self")
        dve_g, pool_g = sem("dve_group"), sem("pool_group")
        rB_s, rT_s = sem("rB_s"), sem("rT_s")
        silu_c, silbc_s, mod_ps, mod_s, gate_s = sem("silu_c"), sem("silbc_s"), sem("mod_ps"), sem("mod_s"), sem("gate_s")
        var_s, std_s, xn_s, xT_ps, hT_s = sem("var_s"), sem("std_s"), sem("xn_s"), sem("xT_ps"), sem("hT_s")
        qk_ps, v_ps, q32_s, qk_used, v_s, piece_s = sem("qk_ps"), sem("v_ps"), sem("q32_s"), sem("qk_used"), sem("v_s"), sem("piece_s")
        piece_out = [sem(f"piece_out{c}") for c in range(NC_)]
        aug0_in = [sem(f"aug0_in{c}") for c in range(NC_)]
        aug_in, aug_free, const_in = sem("aug_in"), sem("aug_free"), sem("const_in")
        s1_ready, s1_free = sem("s1_ready"), sem("s1_free")
        tick_s, nmax_s, nmp_s = sem("tick_s"), sem("nmax_s"), sem("nmp_s")
        s2_ready, exp_done, exp_diag, diag_done = sem("s2_ready"), sem("exp_done"), sem("exp_diag"), sem("diag_done")
        rows_s, rows_in = sem("rows_s"), [sem("rows_in0"), sem("rows_in1")]
        pv_done, yT_pe, yT_dve, rl_s, yN_s, yn_s = sem("pv_done"), sem("yT_pe"), sem("yT_dve"), sem("rl_s"), sem("yN_s"), sem("yn_s")
        v_used, v_ready = sem("v_used"), sem("v_ready")
        wp_s, w2_s = sem("wp_s"), sem("w2_s")
        pj_ps, x2_s = sem("pj_ps"), sem("x2_s")
        lg_ps, lg_s, pe_s, d_s, ed_s = sem("lg_ps"), sem("lg_s"), sem("pe_s"), sem("d_s"), sem("ed_s")
        up_ready, hs_ready, y_ready, y_free = (sem(n) for n in ("up_ready", "hs_ready", "y_ready", "y_free"))
        out_s, stored = sem("out_s"), sem("stored")

        x_v = a["x"].rearrange("(n p) c -> p n c", p=P)
        o_v = a["out"].rearrange("(n p) c -> p n c", p=P)
        qa4 = q_aug[:, :].rearrange("r (b h t) -> r b h t", b=2, h=HG)
        ka4 = k_aug[:, :].rearrange("r (b h t) -> r b h t", b=2, h=HG)
        NSMALL = 8

        block = ctx.enter_context(nc.Block())

        def load_stack(e, g, buf, c0, c1, done):
            t0, t1 = c0 * CW, c1 * CW
            for i in range(3):
                src = q_dram[i].rearrange("(h d) j t -> h (d j) t", d=D)
                e.dma_start(qa4[PAIR * i:PAIR * (i + 1), ds(buf, 1), :, t0:t1].rearrange("r b h t -> r (b h) t"),
                            src[ds(g * HG, HG), :, t0:t1].rearrange("h r t -> r h t")).then_inc(done, 16)
                src = k_dram.rearrange("(h d) j t -> h (d j) t", d=D)
                e.dma_start(ka4[PAIR * i:PAIR * (i + 1), ds(buf, 1), :, t0:t1].rearrange("r b h t -> r (b h) t"),
                            src[ds(g * HG, HG), :, t0:t1].rearrange("h r t -> r h t")).then_inc(done, 16)

        def load_alibi(e, g, buf, done):
            for k, aug in enumerate((qa4, ka4)):
                e.dma_start(aug[ALIBI0:ALIBI0 + 4, ds(buf, 1), :, :].rearrange("r b h t -> r (b h) t"),
                            a["alibi"][k].rearrange("r h t -> r h t")[:, ds(g * HG, HG), :]).then_inc(done, 16)

        @block.sync
        def _(sp):
            for c in range(NC_):
                sp.dma_start(x_sb[:, TPC * c:TPC * (c + 1), :], x_v[:, TPC * c:TPC * (c + 1), :]).then_inc(x_in[c], 16)
            for k in range(2):
                sp.wait_ge(pad_set, 2 * k + 2)
                load_alibi(sp, k, k, const_in)
                sp.dma_start(ka4[MAX0:MAX0 + 3, k, :, :], a["ones3"]).then_inc(const_in, 16)
            for c in range(NC_):
                sp.wait_ge(piece_s, 2 * (c + 1))
                for i in range(3):
                    sp.dma_start(q_dram[i, :, 0:3 - i, c * CW:(c + 1) * CW], pieces[:, c % 2, 0, i:3, :]).then_inc(piece_out[c], 16)
                    if i:
                        sp.dma_start(q_dram[i, :, 3 - i:3, c * CW:(c + 1) * CW], pieces[:, c % 2, 0, 0:i, :]).then_inc(piece_out[c], 16)
                sp.dma_start(k_dram[:, :, c * CW:(c + 1) * CW], pieces[:, c % 2, 1, :, :]).then_inc(piece_out[c], 16)
                sp.wait_ge(piece_out[c], 6 * 16)
                load_stack(sp, 0, 0, c, c + 1, aug0_in[c])

            def group(g, first, last):
                if not last:
                    take(sp, aug_free, 1)
                    nxt = g + 1
                    buf = nxt % 2 if first else sp.snap(nxt % 2)
                    load_stack(sp, nxt, buf, 0, NC_, aug_in)
                    if not first:
                        load_alibi(sp, nxt, buf, aug_in)
                for p in range(-1, NSTEP):
                    for u in turns(p, first, last):
                        take(sp, rows_s, 1)
                        gu = g + u // NC_
                        buf = gu % 2 if isinstance(gu, int) else sp.snap(gu % 2)
                        t0 = (u % NC_) * CW
                        for i in range(3):
                            dst = qa4[MAX0 + i:MAX0 + i + 1, ds(buf, 1), :, t0:t0 + CW]
                            sp.dma_start(dst.rearrange("r b h t -> r (b h) t"),
                                         rows[HG * i:HG * (i + 1), u % 2, :]).then_inc(rows_in[u % 2], 16)

            for dst, src in ((rwT[:, :], a["rwT"]), (tri8[:, :, :], a["tri8"]), (scale_bc[:, :], a["scale"].to_broadcast([P, E]))):
                sp.dma_start(dst, src).then_inc(late_in, 16)
            group(0, True, False)
            with sp.Fori(1, G - 1) as g:
                group(g, False, False)
            take(sp, aug_free, 1)
            for dst, src in ((w1T, a["w1T"]), (w2T, a["w2T"])):
                sp.dma_start(dst, src).then_inc(late_in, 16)
            group(G - 1, False, True)
            for c in range(NC_):
                sp.wait_ge(out_s, c + 1)
                sp.dma_start(o_v[:, TPC * c:TPC * (c + 1), :], x_sb[:, TPC * c:TPC * (c + 1), :]).then_inc(stored, 16)
            sp.wait_ge(stored, 16 * NC_)

        @block.tensor
        def _(pe):
            mm = nc.tensor.matmul
            pe.wait_ge(small_in, 16 * NSMALL)
            pe.wait_ge(silu_c, 1)
            for n, m in enumerate((0, 1, 3, 4)):
                mm(b1[:, 0, n:n + 1], wmod[:, m * C:(m + 1) * C], sil[:, :], start=True, stop=True)
            pe.wait_ge(silbc_s, 1)
            for n, m in enumerate((2, 5)):
                last = mm(b1[:, 1, n * C:(n + 1) * C], silbc[:, :], wmod[:, m * C:(m + 1) * C], start=True, stop=True)
            last.then_inc(mod_ps, 1)

            def turn_tokens(c, out, done):
                for i in range(TPC):
                    last = nc.tensor.transpose(out[:, i * P:(i + 1) * P], xn[:, TPC * c + i, :], ident[:, :])
                last.then_inc(done, 1)

            for c in range(NC_):
                pe.wait_ge(xn_s, c + 1)
                if c >= 2:
                    pe.wait_ge(hT_s, c - 1)
                turn_tokens(c, b2[:, c % 2, :], xT_ps)
                pe.wait_ge(hT_s, c + 1)
                if c == 0:
                    pe.wait_ge(gate_s, 1)
                for n in range(2):
                    if c:
                        pe.wait_ge(q32_s, 2 * (c - 1) + n + 1)
                    mm(b1[:, n, :], wqkv[:, n * C:(n + 1) * C], hT[:, c * CW:(c + 1) * CW], start=True, stop=True).then_inc(qk_ps, 1)
                if c:
                    pe.wait_ge(v_s, c)
                for i in range(TPC):
                    t = (TPC * c + i) * P
                    last = mm(b1[:, 2, i * C:(i + 1) * C], hT[:, t:t + P], wqkv[:, 2 * C:3 * C], start=True, stop=True)
                last.then_inc(v_ps, 1)
            pe.wait_ge(q32_s, 2 * NC_)
            pe.wait_ge(v_s, NC_)
            pe.sem_inc(s1_free, RING1)
            pe.sem_inc(yT_pe, 1)

            def group(g, first, last):
                cur = 0 if first else 1 if last else pe.snap(g % 2)
                nxt = 1 if first else None if last else pe.snap(1 - cur)
                n_task = [0]
                at = [0 if first else TPC * LEAD]
                freed = []
                count = {"exp": 0, "diag": 0}
                exps, diags = [], []

                def stack(aug, n, buf, hh, t, w):
                    if isinstance(buf, int):
                        return aug[0:n, buf, hh, t:t + w]
                    return aug[0:n, ds(buf, 1), hh, t:t + w].rearrange("r b t -> r (b t)")

                def pass1(upto):
                    while at[0] < upto:
                        k = at[0]
                        j, c, r, hh = TASKS[k % NTASK]
                        off = cur if k < NTASK else nxt
                        if first and k < NTASK and k == TPC * START[j]:
                            pe.wait_ge(aug0_in[j], 6 * 16)
                        if first and k == 0:
                            pe.wait_ge(const_in, 4 * 16 + 2 * 16)
                        if k == NTASK:
                            take(pe, aug_in, (6 if first else 8) * 16)
                        n_task[0] += 1
                        pe.wait_ge(s1_free, n_task[0])
                        w = (r + 1) * P if c == j else CW
                        mm(b1[:, k % RING1, 0:w], stack(qa4, ROWS1, off, hh, j * CW + r * P, P), stack(ka4, ROWS1, off, hh, c * CW, w),
                           start=True, stop=True).then_inc(s1_ready, 1)
                        at[0] += 1

                def turn(u):
                    take(pe, nmp_s, 1)
                    slot = len(freed) % RING2
                    wait_slot()
                    out = b2[0:3 * HG, slot, 0:CW // 2].bitcast(bf16)
                    for i in range(TPC):
                        last_ = nc.tensor.transpose(out[:, i * P:(i + 1) * P], nmp[:, u % 2, i, :, :], identb[:, :])
                    last_.then_inc(s2_ready, 1)
                    freed.append(None)

                def wait_slot():
                    k = len(freed) - RING2
                    if k >= 0:
                        if freed[k] is None:
                            k += 1
                        pe.wait_ge(*freed[k])

                def step(p):
                    if p == 0:
                        pass1(TPC * ahead(0, first))
                        for u in turns(-1, first, last):
                            turn(u)
                    lo, hi = at[0], TPC * ahead(min(p + 1, NSTEP), first)
                    if last:
                        hi = min(hi, NTASK)
                    if p < NSTEP:
                        j, kb = STEPS[p]
                        w = width(j, kb)
                        diag = kb >= TPC * j
                        if p == START[j]:
                            take(pe, rows_in[j % 2], 3 * 16)
                        for hh in range(HG):
                            pass1(lo + (hi - lo) * (hh + 1) // HG)
                            wait_slot()
                            ins = mm(b2[:, len(freed) % RING2, 0:w], stack(ka4, ROWS2, cur, hh, kb * P, P), stack(qa4, ROWS2, cur, hh, (j + 1) * CW - w, w),
                                     start=True, stop=True)
                            ins.then_inc(s2_ready, 1)
                            if diag:
                                count["diag"] += 1
                            if w > P:
                                count["exp"] += 1
                            freed.append((exp_done, count["exp"]) if w > P else (diag_done, count["diag"]))
                        exps.append(count["exp"])
                        diags.append(count["diag"])
                        for u in turns(p, first, last):
                            turn(u)
                    if p >= 1:
                        j, kb = STEPS[p - 1]
                        w = width(j, kb)
                        diag = kb >= TPC * j
                        if w > P:
                            pe.wait_ge(exp_done, exps[p - 1])
                        if diag:
                            pe.wait_ge(diag_done, diags[p - 1])
                        if kb == 0:
                            take(pe, yT_pe, 1)
                        if kb % TPC == 0 and kb // TPC == j:
                            take(pe, v_ready, 1)
                        for hh in range(HG):
                            ins = mm(pv[32 * hh:32 * hh + 32, CW - w:CW], v_cur[:, kb, hh, :], probs[:, (p - 1) % 2, hh, 0:w],
                                     start=(kb == 0), stop=(kb == TPC * (j + 1) - 1), skip_group_check=True)
                            if hh == 0 and (p - 1 == 0 or (p - 1 - START[3] in (4, 8, 12))):
                                ins.then_inc(v_used, 1)
                        ins.then_inc(pv_done, 1)

                for p0 in range(0, NSTEP + 1, SECTION):
                    with ExitStack() as part_:
                        if not (first or last):
                            part_.enter_context(pe.Fori(0, 1))
                        for p in range(p0, min(p0 + SECTION, NSTEP + 1)):
                            step(p)
                pe.sem_inc(s1_free, -n_task[0])
                pe.sem_inc(exp_done, -count["exp"])
                pe.sem_inc(diag_done, -count["diag"])
            pe.sem_inc(aug_free, 1)
            group(0, True, False)
            pe.sem_inc(aug_free, 1)
            with pe.Fori(1, G - 1) as g:
                group(g, False, False)
                pe.sem_inc(aug_free, 1)
            group(G - 1, False, True)

            pe.wait_ge(wp_s, 1)
            for c in range(NC_):
                pe.wait_ge(yn_s, G * NC_)
                for i in range(TPC):
                    t = (TPC * c + i) * P
                    for g in range(G):
                        last = mm(b1[:, c, i * C:(i + 1) * C], yn[:, g * T + t:g * T + t + P], wproj[:, g, :], start=(g == 0), stop=(g == G - 1))
                last.then_inc(pj_ps, 1)
            for c in range(NC_):
                pe.wait_ge(xn_s, NC_ + c + 1)
                if c >= 2:
                    pe.wait_ge(hT_s, NC_ + c - 1)
                turn_tokens(c, b2[:, c % 2, :], xT_ps)
            for c in range(NC_):
                pe.wait_ge(hT_s, NC_ + c + 1)
                for i in range(TPC):
                    t = (TPC * c + i) * P
                    last = mm(pv[:, (TPC * c + i) * E:(TPC * c + i + 1) * E], hT[:, t:t + P], rwT[:, :], start=True, stop=True)
            last.then_inc(lg_ps, 1)

            pe.wait_ge(late_in, 5 * 16)
            pe.wait_ge(x2_s, NC_)
            pe.wait_ge(w2_s, 8)
            pe.sem_inc(hs_ready, RING1)
            pe.sem_inc(y_free, 2)
            with pe.Fori(0, NC_) as c:
                t0 = pe.snap(c * CW)

                def down(e):
                    pe.wait_ge(hs_ready, RING1 + FC * (e + 1))
                    pe.wait_ge(y_free, e + 1)
                    for i in range(TPC):
                        for f in range(FC):
                            last = mm(b2[:, e % 2, i * C:(i + 1) * C], hs[:, e % 2, f, i * P:(i + 1) * P], w2T[:, e * FC + f, :],
                                      start=(f == 0), stop=(f == FC - 1))
                    last.then_inc(y_ready, 1)

                for e in range(E):
                    for f in range(FC):
                        n = e * FC + f
                        pe.wait_ge(hs_ready, n + 1)
                        mm(b1[:, n % RING1, :], w1T[:, n * P:(n + 1) * P], hT[:, ds(t0, CW)], start=True, stop=True).then_inc(up_ready, 1)
                    if e:
                        down(e - 1)
                down(E - 1)
                pe.sem_inc(hs_ready, -E * FC)
                pe.sem_inc(y_free, -E)

        @block.vector
        def _(dve):
            own = Own(dve, dve_s)
            own.inc(nc.vector.memset(ones[:, :], 1.0))
            dve.wait_ge(silu_c, 1)
            own.wait()
            nc.vector.tensor_scalar(silbc[:, :], ones[:, :], sil[:, 0:1], None, ALU.mult).then_inc(silbc_s, 1)
            dve.wait_ge(small_in, 16 * NSMALL)
            own.inc(nc.vector.tensor_scalar(bqk[:, 0:1], bqk[:, 0:1], D ** -0.5, None, ALU.mult))
            for n in range(NT):
                if n % TPC == 0:
                    dve.wait_ge(x_in[n // TPC], 16)
                own.inc(nc.vector.bn_stats(stats[:, n, :], x_sb[:, n, :]))
            own.wait()
            for n in range(NT):
                last = nc.vector.bn_aggr(mv[:, n, :], stats[:, n, :])
            last.then_inc(var_s, 1)
            dve.wait_ge(mod_ps, 1)
            own.inc(nc.vector.tensor_copy(modc[:, 0:4:2], b1[:, 0, 0:4:2]))
            own.inc(nc.vector.tensor_scalar(modc[:, 1:4:2], b1[:, 0, 1:4:2], 1.0, None, ALU.add))
            g_ps = b1[:, 1, 0:2 * C].rearrange("p (a c) -> p a c", a=2)
            own.inc(nc.vector.tensor_scalar(gsgn[:, :, :], g_ps, 0.0, 2.0, ALU.is_ge, ALU.mult))
            own.inc(nc.vector.tensor_scalar(gabs[:, :, :], g_ps, -1.0, None, ALU.mult))
            own.wait()
            own.inc(nc.vector.tensor_tensor(gabs[:, :, :], g_ps, gabs[:, :, :], ALU.max))
            own.wait()
            own.inc(nc.vector.tensor_scalar(gabs[:, :, :], gabs[:, :, :], 0.25, None, ALU.max))
            own.wait()
            nc.vector.scalar_tensor_tensor(gate[:, :, :], gsgn[:, :, :], -1.0, gabs[:, :, :], ALU.add, ALU.mult).then_inc(gate_s, 1)

            def normalise(c):
                for i in range(TPC):
                    n = TPC * c + i
                    last = nc.vector.tensor_scalar(xn[:, n, :], x_sb[:, n, :], mv[:, n, 0:1], rstd[:, n:n + 1], ALU.subtract, ALU.mult)
                last.then_inc(xn_s, 1)

            dve.wait_ge(std_s, 1)
            own.inc(nc.vector.reciprocal(rstd[:, :], std[:, :]))
            own.wait()
            for c in range(NC_):
                normalise(c)
            for c in range(NC_):
                for n in range(2):
                    dve.wait_ge(q32_s, 2 * c + n + 1)
                    own.inc(nc.vector.tensor_tensor(res[:, n, :], q32[:, n, :], pieces[:, c % 2, n, 0, :], ALU.subtract))
                    own.wait()
                    own.inc(nc.vector.tensor_copy(pieces[:, c % 2, n, 1, :], res[:, n, :]))
                    own.wait()
                    nc.vector.tensor_tensor(pieces[:, c % 2, n, 2, :], res[:, n, :], pieces[:, c % 2, n, 1, :], ALU.subtract).then_inc(piece_s, 1)
                dve.wait_ge(v_ps, c + 1)
                nc.vector.tensor_tensor(v_all[:, TPC * c:TPC * (c + 1), :], b1[:, 2, :].rearrange("p (b c) -> p b c", b=TPC),
                                        bv_bc[:, None, :].to_broadcast([P, TPC, C]), ALU.add).then_inc(v_s, 1)

            def norm_a(j):
                take(dve, yT_dve, 1)
                k = j % 2
                mine.inc(nc.vector.transpose(yB[:, k, :, :].rearrange("p b q -> p (b q)"), yT[:, k, :]))
                mine.wait()
                nc.vector.reciprocal(rl[:, k, :], yB[:, k, :, D]).then_inc(rl_s, 1)

            def norm_b(j):
                take(dve, rB_s, 1)
                k = j % 2
                nc.vector.transpose(yB[:, k, :, :].rearrange("p b q -> p (b q)"), yN[:, k, :, :].rearrange("p b q -> p (b q)")).then_inc(rT_s, 1)

            mine = Own(dve, dve_g)

            def group(first, last):
                n_task, at = 0, 0 if first else TPC * LEAD
                for p in range(-1, NSTEP):
                    if p >= 0:
                        for base, j in ((5, 3), (5, 0), (START[2] + 1, 1), (START[3] + 1, 2)):
                            if p == base and not (first and j == 3):
                                norm_a(j)
                            if p == base + 2 and not (first and j == 3):
                                norm_b(j)
                    upto = TPC * ahead(p + 1, first)
                    if last:
                        upto = min(upto, NTASK)
                    while at < upto:
                        k = at % NTASK
                        j, c, r, hh = TASKS[k]
                        n_task += 1
                        dve.wait_ge(s1_ready, n_task)
                        dst = part[:, j % 2, r * HG + hh, c:c + 1]
                        if c == j:
                            w = (r + 1) * P
                            nc.vector.tensor_tensor_reduce(out=junk[:, k % RING1, 0:w], in0=b1[:, k % RING1, 0:w], in1=mask[:, CW - w:CW],
                                                           scale=1.0, scalar=3 * BIG, op0=ALU.add, op1=ALU.max,
                                                           accum_out=dst).then_inc(s1_free, 1)
                        else:
                            nc.vector.tensor_reduce(dst, b1[:, k % RING1, :], AX.X, ALU.max).then_inc(s1_free, 1)
                        at += 1
                        if k + 1 == TPC * START[j + 1]:
                            mine.inc(nc.vector.memset(tick[:, 0:1], 0.0))
                            mine.wait()
                            nc.vector.tensor_reduce(nmax[:, j % 2, :, :].rearrange("p r h -> p (r h)"), part[:, j % 2, :, 0:j + 1], AX.X, ALU.max,
                                                    negate=True).then_inc(nmax_s, 1)
                dve.sem_inc(s1_ready, -n_task)
                mine.reset()

            group(True, False)
            with dve.Fori(1, G - 1):
                group(False, False)
            group(False, True)
            norm_a(3)
            norm_b(3)
            mine.reset()

            for c in range(NC_):
                dve.wait_ge(pj_ps, c + 1)
                xc = x_sb[:, TPC * c:TPC * (c + 1), :]
                own.inc(nc.vector.tensor_tensor(xc, b1[:, c, :].rearrange("p (b c) -> p b c", b=TPC), xc, ALU.add))
                own.wait()
                for i in range(TPC):
                    own.inc(nc.vector.bn_stats(stats[:, TPC * c + i, :], x_sb[:, TPC * c + i, :]))
            own.wait()
            nc.vector.memset(tick[:, 1:2], 0.0).then_inc(x2_s, NC_)
            for n in range(NT):
                last = nc.vector.bn_aggr(mv[:, n, :], stats[:, n, :])
            last.then_inc(var_s, 1)
            dve.wait_ge(std_s, 2)
            own.inc(nc.vector.reciprocal(rstd[:, :], std[:, :]))
            own.wait()
            for c in range(NC_):
                normalise(c)
            V = nc.vector
            dve.wait_ge(lg_ps, 1)
            lps = pv[:, 0:NT * E].rearrange("p (n e) -> p n e", e=E)

            def step(ins):
                own.inc(ins)
                own.wait()

            step(V.tensor_reduce(lmax[:, :], lps, AX.X, ALU.max))
            V.tensor_tensor(lg[:, :, :], lps, lmax[:, :].unsqueeze(2).to_broadcast([P, NT, E]), ALU.subtract).then_inc(lg_s, 1)
            dve.wait_ge(pe_s, 1)
            step(V.tensor_reduce(psm[:, :], pr[:, :, :], AX.X, ALU.add))
            step(V.reciprocal(psm[:, :], psm[:, :]))
            step(V.tensor_tensor(pr[:, :, :], pr[:, :, :], psm[:, :].unsqueeze(2).to_broadcast([P, NT, E]), ALU.mult))
            mine_e = pr[:, :, :].unsqueeze(3).to_broadcast([P, NT, E, E])
            other_e = pr[:, :, :].unsqueeze(2).to_broadcast([P, NT, E, E])
            own.inc(V.tensor_tensor(gt[:, :, :, :], other_e, mine_e, ALU.is_gt))
            step(V.tensor_tensor(eq[:, :, :, :], other_e, mine_e, ALU.is_equal))
            step(V.tensor_tensor(eq[:, :, :, :], eq[:, :, :, :], tri8[:, None, :, :].to_broadcast([P, NT, E, E]), ALU.mult))
            step(V.tensor_tensor(gt[:, :, :, :], gt[:, :, :, :], eq[:, :, :, :], ALU.add))
            step(V.tensor_reduce(rank[:, :, :], gt[:, :, :, :], AX.X, ALU.add))
            for k in range(TOPK):
                step(V.tensor_scalar(hot[:, k, :, :], rank[:, :, :], float(k), None, ALU.is_equal))
                step(V.tensor_tensor(lg[:, :, :], hot[:, k, :, :], pr[:, :, :], ALU.mult))
                step(V.tensor_reduce(ptop[:, k, :], lg[:, :, :], AX.X, ALU.add))
            V.tensor_tensor(wtop[:, 0, :], ptop[:, 1, :], ptop[:, 0, :], ALU.subtract).then_inc(d_s, 1)
            dve.wait_ge(ed_s, 1)
            step(V.tensor_scalar(psm[:, :], wtop[:, 1, :], 1.0, None, ALU.add))
            step(V.reciprocal(wtop[:, 0, :], psm[:, :]))
            step(V.tensor_tensor(wtop[:, 1, :], wtop[:, 1, :], wtop[:, 0, :], ALU.mult))
            for k in range(TOPK):
                step(V.tensor_tensor(hot[:, k, :, :], hot[:, k, :, :], wtop[:, k, :].unsqueeze(2).to_broadcast([P, NT, E]), ALU.mult))
            step(V.tensor_tensor(comb[:, :, :], hot[:, 0, :, :], hot[:, 1, :, :], ALU.add))
            step(V.tensor_tensor(comb[:, :, :], comb[:, :, :], scale_bc[:, None, :].to_broadcast([P, NT, E]), ALU.mult))
            cf = comb[:, :, :].rearrange("p n e -> p (n e)")
            xf = x_sb[:, :, :].rearrange("p n c -> p (n c)")
            with dve.Fori(0, NC_) as c:
                n0 = dve.snap(c * (TPC * E))
                t0 = dve.snap(c * CW)
                for e in range(E):
                    dve.wait_ge(y_ready, e + 1)
                    for i in range(TPC):
                        y, w = b2[:, e % 2, i * C:(i + 1) * C], cf[:, ds(n0 + (i * E + e), 1)]
                        if e == 1:
                            last = V.tensor_scalar(accO[:, i, :], y, w, None, ALU.mult)
                        else:
                            acc = accO[:, i, :] if e % 2 else xf[:, ds(t0 + i * C, C)]
                            last = V.scalar_tensor_tensor(acc, y, w, acc, ALU.mult, ALU.add)
                    last.then_inc(y_free, 1)
                dve.sem_inc(y_ready, -E)
                mine.inc(V.memset(tick[:, 0:1], 0.0))
                mine.wait()
                V.tensor_tensor(xf[:, ds(t0, CW)], xf[:, ds(t0, CW)], accO[:, :, :].rearrange("p b c -> p (b c)"), ALU.add).then_inc(out_s, 1)
                mine.inc(V.memset(tick[:, 2:3], 0.0))
                mine.reset()

        @block.scalar
        def _(act):
            small = [(ccol[:, :], a["ccol"]), (wmod[:, :], a["wmod"]), (ident[:, :], a["ident"]), (wqkv[:, :], a["wqkv"]),
                     (bqk[:, :], a["bqk"]), (bv_bc[:, :], a["bv"].to_broadcast([P, C])), (mask[:, :], a["mask"]),
                     (wproj[:, :, :], a["wproj"])]
            for dst, src in small:
                act.dma_start(dst, src).then_inc(small_in, 16)
            act.wait_ge(small_in, 16 * len(small))
            nc.scalar.activation(sil[:, :], ccol[:, :], ACT.Silu).then_inc(silu_c, 1)
            own = Own(act, act_s)

            def deviations(k):
                act.wait_ge(var_s, k + 1)
                own.inc(nc.scalar.activation(std[:, :], mv[:, :, 1], ACT.Copy, bias=EPS))
                own.wait()
                nc.scalar.activation(std[:, :], std[:, :], ACT.Sqrt).then_inc(std_s, 1)

            def features(c, k):
                act.wait_ge(xT_ps, NC_ * k + c + 1)
                nc.scalar.activation(hT[:, c * CW:(c + 1) * CW], b2[:, c % 2, :], ACT.Identity,
                                     bias=modc[:, 2 * k:2 * k + 1], scale=modc[:, 2 * k + 1:2 * k + 2]).then_inc(hT_s, 1)

            deviations(0)
            act.wait_ge(gate_s, 1)
            for c in range(NC_):
                features(c, 0)
                for n in range(2):
                    act.wait_ge(qk_ps, 2 * c + n + 1)
                    if c:
                        act.wait_ge(piece_s, 2 * (c - 1) + n + 1)
                    if c >= 2 and n == 0:
                        act.wait_ge(piece_out[c - 2], 6 * 16)
                    own.inc(nc.scalar.activation(q32[:, n, :], b1[:, n, :], ACT.Identity, bias=bqk[:, n:n + 1],
                                                 scale=D ** -0.5 if n == 0 else 1.0))
                    own.wait()
                    nc.scalar.activation(pieces[:, c % 2, n, 0, :], q32[:, n, :], ACT.Copy).then_inc(q32_s, 1)

            def group(first, last):
                n2 = 0

                def turned(u, n2):
                    act.wait_ge(s2_ready, n2)
                    nc.scalar.activation(rows[:, u % 2, :], b2[0:3 * HG, (n2 - 1) % RING2, 0:CW // 2].bitcast(bf16), ACT.Copy).then_inc(rows_s, 1)

                for u in turns(-1, first, last):
                    n2 += 1
                    turned(u, n2)
                for p in range(NSTEP + 1):
                    if p < NSTEP:
                        j, kb = STEPS[p]
                        w = width(j, kb)
                        diag = kb >= TPC * j
                        if p >= 2:
                            act.wait_ge(pv_done, p - 1)
                        for hh in range(HG):
                            n2 += 1
                            act.wait_ge(s2_ready, n2)
                            bank = b2[:, (n2 - 1) % RING2, :]
                            cut = P if diag else 0
                            if diag:
                                nc.scalar.activation(probs[:, p % 2, hh, 0:P], bank[:, 0:P], ACT.Exp).then_inc(exp_diag, 1)
                            if w > cut:
                                nc.scalar.activation(probs[:, p % 2, hh, cut:w], bank[:, cut:w], ACT.Exp).then_inc(exp_done, 1)
                        for u in turns(p, first, last):
                            n2 += 1
                            turned(u, n2)
                    if p in START[1:]:
                        j = START.index(p) - 1
                        act.wait_ge(pv_done, p)
                        nc.scalar.activation(yT[:, j % 2, :], pv[:, :], ACT.Copy).then_inc(yT_dve, 1)
                        nc.scalar.activation(tick[:, 8 + j:9 + j], ident[:, 0:1], ACT.Copy).then_inc(yT_pe, 1)
                act.sem_inc(s2_ready, -n2)
                act.sem_inc(pv_done, -NSTEP)

            group(True, False)
            with act.Fori(1, G - 1):
                group(False, False)
            group(False, True)

            deviations(1)
            for c in range(NC_):
                features(c, 1)
            act.wait_ge(lg_s, 1)
            nc.scalar.activation(pr[:, :, :], lg[:, :, :], ACT.Exp).then_inc(pe_s, 1)
            act.wait_ge(d_s, 1)
            nc.scalar.activation(wtop[:, 1, :], wtop[:, 0, :], ACT.Exp).then_inc(ed_s, 1)
            with act.Fori(0, NC_):
                for n in range(E * FC):
                    e, f = divmod(n, FC)
                    act.wait_ge(up_ready, n + 1)
                    nc.scalar.activation(hs[:, e % 2, f, :], b1[:, n % RING1, :], ACT.Silu).then_inc(hs_ready, 1)
                act.sem_inc(up_ready, -E * FC)

        @block.gpsimd
        def _(pool):
            own = Own(pool, pool_s)
            u32 = mybir.dt.uint32
            half = HG * T
            for k in range(2):
                for aug in (q_aug, k_aug):
                    nc.gpsimd.memset(aug[PAD0:ROWS2, k * half:(k + 1) * half].bitcast(u32), 0).then_inc(pad_set, 1)
            pool.wait_ge(pad_set, 4)
            own.inc(nc.gpsimd.memset(v_cur[:, :, :, :], 0.0))
            own.wait()
            own.inc(nc.gpsimd.memset(v_cur[:, :, :, D:2 * D], 1.0))
            pool.wait_ge(small_in, 16 * NSMALL)
            own.inc(nc.gpsimd.tensor_copy(identb[:, :], ident[:, :]))
            pool.wait_ge(gate_s, 1)
            nc.gpsimd.tensor_tensor(wproj[:, :, :], wproj[:, :, :], gate[:, 0:1, :].to_broadcast([P, G, C]), ALU.mult).then_inc(wp_s, 1)
            own.wait()

            def values(q, g):
                b = slice(TPC * q, TPC * (q + 1))
                src = v_all[:, b, ds(g * HG * D, HG * D)].rearrange("p b (h d) -> p b h d", d=D)
                nc.gpsimd.tensor_copy(v_cur[:, b, :, 0:D], src).then_inc(v_ready, 1)

            for q in range(3):
                pool.wait_ge(v_s, q + 1)
                values(q, 0)
            pool.wait_ge(v_s, NC_)
            mine = Own(pool, pool_g)

            def cut_maxima(u):
                take(pool, nmax_s, 1)
                k = u % 2
                mine.inc(nc.gpsimd.tensor_copy(nmp[:, k, :, 0, :], nmax[:, k, :, :]))
                mine.wait()
                mine.inc(nc.gpsimd.tensor_tensor(nres[:, k, :, :], nmax[:, k, :, :], nmp[:, k, :, 0, :], ALU.subtract))
                mine.wait()
                mine.inc(nc.gpsimd.tensor_copy(nmp[:, k, :, 1, :], nres[:, k, :, :]))
                mine.wait()
                nc.gpsimd.tensor_tensor(nmp[:, k, :, 2, :], nres[:, k, :, :], nmp[:, k, :, 1, :], ALU.subtract).then_inc(nmp_s, 1)

            def spread(j):
                take(pool, rl_s, 1)
                k = j % 2
                nc.gpsimd.tensor_copy(yN[:, k, :, :], rl[:, k, :].unsqueeze(2).to_broadcast([P, CW // 32, 32])).then_inc(rB_s, 1)

            def normal(j, g):
                take(pool, rT_s, 1)
                k = j % 2
                nc.gpsimd.tensor_tensor(yn[:, ds(g * T + j * CW, CW)], yT[:, k, :], yB[:, k, :, :].rearrange("p b q -> p (b q)"),
                                        ALU.mult).then_inc(yn_s, 1)

            def group(g, first, last):
                n_diag = 0
                for p in range(-1, NSTEP + 1):
                    if p == 1:
                        take(pool, v_used, 1)
                        values(3, g)
                    for u in turns(p, first, last):
                        cut_maxima(u)
                    for base, j in ((5, 3), (5, 0), (START[2] + 1, 1), (START[3] + 1, 2)):
                        if not (first and j == 3):
                            if p == base + 1:
                                spread(j)
                            if p == base + 3:
                                normal(j, g - 1 if j == 3 else g)
                    if 0 <= p < NSTEP and STEPS[p][1] >= TPC * STEPS[p][0]:
                        for hh in range(HG):
                            n_diag += 1
                            pool.wait_ge(exp_diag, n_diag)
                            t = probs[:, p % 2, hh, 0:P]
                            nc.gpsimd.affine_select(out=t, in_=t, compare_op=ALU.is_ge, fill=0.0, base=0, pattern=[[1, P]],
                                                    channel_multiplier=-1).then_inc(diag_done, 1)
                    for q in range(3):
                        if p == START[3] + TPC * (q + 1) + 1:
                            take(pool, v_used, 1)
                            if not last:
                                values(q, g + 1)
                    if last and START[3] + 2 <= p < START[3] + 10:
                        k = p - START[3] - 2
                        if k == 0:
                            pool.wait_ge(late_in, 5 * 16)
                        w = w2T[:, 4 * k:4 * k + 4, :]
                        nc.gpsimd.tensor_tensor(w, w, gate[:, 1:2, :].to_broadcast([P, 4, C]), ALU.mult).then_inc(w2_s, 1)
                pool.sem_inc(exp_diag, -n_diag)
                mine.reset()

            group(0, True, False)
            with pool.Fori(1, G - 1) as g:
                group(g, False, False)
            group(G - 1, False, True)
            spread(3)
            normal(3, G - 1)


def kernel(L0_attn_x, L0_attn_W_attn, L0_attn_b_attn, L0_attn_W_proj, L0_attn_b_proj, L0_ffn_router_w, L0_ffn_w1, L0_ffn_w2,
           L0_ffn_expert_scale, L0_c, L0_wmod):
    import ml_dtypes
    import concourse.bacc as bacc
    from concourse.bass_utils import run_bass_kernel_spmd

    f32 = np.float32
    cont = np.ascontiguousarray
    wproj = np.zeros((HG, 32, G, C), f32)
    wproj[:, 0:D] = np.asarray(L0_attn_W_proj).reshape(G, HG, D, C).transpose(1, 2, 0, 3)
    wproj[0, D, 0] = np.asarray(L0_attn_b_proj)
    slope = (2.0 ** -np.arange(1, H + 1)).astype(f32)[:, None]
    t = np.arange(T)
    one = np.ones((H, T), f32)
    alibi = np.stack([np.stack([-P * slope * (t // P), one, -slope * (t % P), one]),
                      np.stack([one, P * slope * (t // P), one, slope * (t % P)])]).astype(ml_dtypes.bfloat16)
    q, k = np.arange(P)[:, None], np.arange(P)[None, :]
    mask = np.zeros((P, CW), f32)
    mask[:, CW - P:] = np.where(k > q, BIG, 0.0)
    ee = np.arange(E)
    arrays = {
        "x": cont(np.asarray(L0_attn_x).reshape(T, C)),
        "wqkv": cont(L0_attn_W_attn),
        "bqk": cont(np.asarray(L0_attn_b_attn)[:2 * C].reshape(2, C).T),
        "bv": cont(np.asarray(L0_attn_b_attn)[2 * C:].reshape(1, C)),
        "wproj": wproj.reshape(P, G, C),
        "rwT": cont(np.asarray(L0_ffn_router_w).T),
        "w1T": cont(np.asarray(L0_ffn_w1).transpose(2, 0, 1).reshape(C, E * F)),
        "w2T": cont(np.asarray(L0_ffn_w2).reshape(E, C, FC, P).transpose(3, 0, 2, 1).reshape(P, E * FC, C)),
        "scale": cont(np.asarray(L0_ffn_expert_scale).reshape(1, E)),
        "ccol": cont(np.asarray(L0_c).reshape(C, 1)),
        "wmod": cont(L0_wmod),
        "ident": np.eye(P, dtype=f32),
        "mask": mask,
        "alibi": alibi,
        "ones3": np.ones((3, HG, T), ml_dtypes.bfloat16),
        "tri8": cont(np.broadcast_to((ee[None, :] < ee[:, None]).astype(f32), (P, E, E))),
    }
    nc = bacc.Bacc("TRN2", target_bir_lowering=False, num_devices=1)
    aps = {n: nc.dram_tensor(f"in_{n}", v.shape, mybir.dt.from_np(v.dtype), kind="ExternalInput").ap() for n, v in arrays.items()}
    aps["out"] = nc.dram_tensor("out_0", (T, C), mybir.dt.float32, kind="ExternalOutput").ap()
    build(nc, aps)
    r = run_bass_kernel_spmd(nc, [{f"in_{n}": v for n, v in arrays.items()}], core_ids=[0])
    return np.asarray(r.results[0]["out_0"]).reshape(1, T, C)
```

```python
from contextlib import ExitStack

import numpy as np

import concourse.bass as bass
from concourse import mybir

T, C, H, D = 2048, 128, 16, 8
P = 128
NT = T // P
CW = 512
NC_ = T // CW
TPC = CW // P
HG = 4
G = H // HG
E, F, TOPK = 8, 512, 2
FC = F // P
EPS = 1e-5
BIG = -1e30

PAIR = 3 * D
ALIBI0 = 3 * PAIR
MAX0 = 93
ROWS1, ROWS2 = MAX0, MAX0 + 3
PAD0 = 64

STEPS = [(j, kbs) for j in range(NC_) for kbs in [[kb] for kb in range(TPC * j)] + [[TPC * j], [TPC * j + 1, TPC * j + 3], [TPC * j + 2]]]
NSTEP = len(STEPS)
START = [[s[0] for s in STEPS].index(j) for j in range(NC_)] + [NSTEP]
TASKS = [(j, c, r, hh) for j in range(NC_) for c in range(j + 1) for r in range(TPC) for hh in range(HG)]
TSTART = [TPC * HG * j * (j + 1) // 2 for j in range(NC_ + 1)]
NTASK = len(TASKS)
LEAD = 88
FIRST_LEAD = 16
SETTLE = 8
SECTION = 4
RING1, RING2 = 4, 3


def width(j, sb):
    return CW - P * max(0, sb - TPC * j)


OVER, VECTOR = 60, 2.45
PASS2 = [HG * sum(width(j, kb) for kb in kbs) for j, kbs in STEPS]
PASS2_END = [sum(PASS2[:p]) for p in range(NSTEP + 1)]


def task_width(k):
    j, c, r, _ = TASKS[k % NTASK]
    return (r + 1) * P if c == j else CW


def vector_work(k):
    return sum(task_width(i) + OVER for i in range(k))


def plan(first):
    if first:
        knots = [(PASS2_END[START[j]], vector_work(TSTART[j + 1] + SETTLE + (12 if j else FIRST_LEAD))) for j in range(NC_)]
        knots.append((PASS2_END[NSTEP], vector_work(NTASK + LEAD)))
    else:
        knots = [(0, vector_work(LEAD)), (PASS2_END[NSTEP], vector_work(NTASK + LEAD))]
    k, rows_ = 0 if first else LEAD, []
    done2 = done1 = 0
    for p in range(NSTEP):
        row = []
        for hh in range(HG):
            x = PASS2_END[p] + hh * PASS2[p] // HG
            for (x0, y0), (x1, y1) in zip(knots, knots[1:]):
                if x0 <= x <= x1:
                    want = y0 + (y1 - y0) * (x - x0) / (x1 - x0)
            while k < NTASK + LEAD and vector_work(k + 1) <= want:
                k += 1
            if p == NSTEP - 1 and hh == HG - 1:
                k = NTASK + LEAD
            row.append(k)
        rows_.append(row)
    return rows_


PLAN = {first: plan(first) for first in (True, False)}


def turns(p, first, last):
    found = []
    for u in range(2 * NC_ if not last else NC_):
        end = TSTART[u % NC_ + 1] + NTASK * (u // NC_)
        if first and u == 0:
            at = -1
        elif end + SETTLE <= (0 if first else LEAD):
            continue
        else:
            steps = [q for q in range(NSTEP) if PLAN[first][q][-1] >= end + SETTLE]
            if not steps:
                continue
            at = steps[0]
        if at == p:
            found.append(u)
    return found


NORM_AT = ((2, 3), (START[1] + 2, 0), (START[2] + 1, 1), (START[3] + 1, 2))

PROJECT = {19: 0, 20: 1, 27: 2}
TURN = {22: 0, 23: 1, 30: 2}
LOGITS = {24: 0, 25: 1, 32: 2}
ROUTE = {26: 0, 29: 1, 33: 2}
ROUTE_EXP = {27: 0, 32: 1}
W1_AT = [4, 6, 8, 10, 12, 14, 16, 18]
LAST_WAY = {2: "project", 3: "turn", 4: "logits"}


def take(e, s, n):
    e.wait_ge(s, n)
    e.sem_inc(s, -n)


class Own:

    def __init__(self, e, s):
        self.e, self.s, self.n = e, s, 0

    def inc(self, ins):
        self.n += 1
        ins.then_inc(self.s, 1)
        return self.n

    def wait(self, n=None):
        self.e.wait_ge(self.s, self.n if n is None else n)

    def reset(self):
        self.wait()
        self.e.sem_inc(self.s, -self.n)
        self.n = 0


def build(nc, a):
    fp32, bf16, fp32r = mybir.dt.float32, mybir.dt.bfloat16, mybir.dt.float32r
    ALU, ACT, AX = mybir.AluOpType, mybir.ActivationFunctionType, mybir.AxisListType
    ds = bass.ds
    with ExitStack() as ctx:
        def sb(name, shape, dt=fp32):
            return ctx.enter_context(nc.sbuf_tensor(name, shape, dt))

        def under(name, shape, dt=fp32):
            with nc.sbuf_tensor(name, shape, dt) as t:
                return t

        def sem(name):
            return ctx.enter_context(nc.semaphore(name))

        x_sb = sb("x_sb", [P, NT, C])
        ident = sb("ident_sb", [P, P])
        mask = sb("mask_sb", [P, CW])
        wqkv = sb("wqkv", [P, 3 * C])
        bqk = sb("bqk", [P, 2])
        bv_bc = sb("bv_bc", [P, C])
        wproj = sb("wproj_sb", [P, G, C])
        ccol = sb("ccol", [P, 1])
        probs = sb("probs", [P, 2, HG, CW])
        early = probs[:, :, :, :].rearrange("p k h t -> p (k h t)")
        wmod = early[:, 0:6 * C]
        rwT = sb("rwT_sb", [P, E])
        scale_bc = sb("scale_bc", [P, E])
        tri8 = sb("tri8_sb", [P, E, E])
        sil = sb("sil", [P, 1])
        ones = early[:, 6 * C:7 * C]
        silbc = early[:, 7 * C:8 * C]
        modc = sb("modc", [P, 4])
        gsgn = early[:, 8 * C:10 * C].rearrange("p (a c) -> p a c", a=2)
        gabs = early[:, 10 * C:12 * C].rearrange("p (a c) -> p a c", a=2)
        gate = sb("gate", [P, 2, C])
        stats = sb("stats", [P, NT, 6])
        mv = sb("mv", [P, NT, 2])
        rstd = sb("rstd", [P, NT])
        neg_half = sb("neg_half", [P, TPC])
        xn = sb("xn", [P, NT, C])
        hT = under("hT", [P, T])
        h_lo = sb("h_lo", [P, T], fp32r)
        h_hi = sb("h_hi", [P, T], fp32r)
        w1_hi = sb("w1_hi", [P, E * F], fp32r)
        q32 = sb("q32", [P, 2, CW])
        res = sb("res", [P, 2, CW])
        pieces = sb("pieces", [P, 2, 2, 3, CW], bf16)
        v_all = xn
        v_cur = sb("v_cur", [P, NT, HG, 32])
        q_aug = under("q_aug", [P, 2 * HG * T], bf16)
        w1T = under("w1T_sb", [P, E * F])
        w1_lo = sb("w1_lo", [P, E * F], fp32r)
        sb("q_aug_1", [P, HG * T], bf16)
        k_aug = sb("k_aug", [P, 2 * HG * T], bf16)
        w2T = k_aug[:, 0:HG * T].bitcast(fp32).rearrange("p (n c) -> p n c", c=C)
        part = sb("part", [P, 2, TPC * HG, NC_])
        junk = sb("junk", [P, RING1, CW], bf16)
        nmax = sb("nmax", [P, 2, TPC, HG])
        nres = sb("nres", [P, 2, TPC, HG])
        nmp = sb("nmp", [P, 2, TPC, 3, HG], bf16)
        identb = sb("identb", [P, P], bf16)
        maskT = sb("maskT_sb", [P, P], bf16)
        rows = sb("rows", [3 * HG, 2, CW], bf16)
        tick = sb("tick", [P, 32])
        yT = q32
        yB = res[:, :, :].rearrange("p k (b q) -> p k b q", q=32)
        late = pieces[:, :, :, :, :].rearrange("p a b c t -> p (a b c t)").bitcast(fp32)
        yN = late[:, 0:2 * CW].rearrange("p (k b q) -> p k b q", k=2, q=32)
        rl = sb("rl", [P, 2, CW // 32])
        yn = sb("yn", [P, G * T])
        lmax = sb("lmax", [P, NT])
        lraw, lg, pr = (wqkv[:, k * P:(k + 1) * P].rearrange("p (n e) -> p n e", e=E) for k in range(3))
        psm = sb("psm", [P, NT])
        ptop = sb("ptop", [P, 2, NT])
        gt = late[:, 2 * CW:4 * CW].rearrange("p (n e f) -> p n e f", e=E, f=E)
        eq = late[:, 4 * CW:6 * CW].rearrange("p (n e f) -> p n e f", e=E, f=E)
        rank = sb("rank", [P, NT, E])
        hot = sb("hot", [P, 2, NT, E])
        wtop = sb("wtop", [P, 2, NT])
        comb = sb("comb", [P, NT, E])
        hs = probs
        accO = mask[:, :].rearrange("p (i c) -> p i c", c=C)

        b1 = ctx.enter_context(nc.psum_tensor("b1", [P, RING1, CW], fp32))
        b2 = ctx.enter_context(nc.psum_tensor("b2", [P, RING2, CW], fp32))
        pv = ctx.enter_context(nc.psum_tensor("pv", [P, CW], fp32))

        q_dram = nc.dram_tensor("q_scratch", (3, P, 3, T), bf16, kind="Internal").ap()
        k_dram = nc.dram_tensor("k_scratch", (P, 3, T), bf16, kind="Internal").ap()

        x_in = [sem(f"x_in{c}") for c in range(NC_)]
        c_in, wmod_in, w_in, mask_in, late_in = sem("c_in"), sem("wmod_in"), sem("w_in"), sem("mask_in"), sem("late_in")
        modc_s, bqk_s, gate_ps = sem("modc_s"), sem("bqk_s"), sem("gate_ps")
        pad_set, pads_set = sem("pad_set"), sem("pads_set")
        dve_s, act_s, pool_s = sem("dve_self"), sem("act_self"), sem("pool_self")
        dve_g, pool_g = sem("dve_group"), sem("pool_group")
        rB_s, rT_s = sem("rB_s"), sem("rT_s")
        silu_c, silbc_s, mod_ps, mod_s, gate_s = sem("silu_c"), sem("silbc_s"), sem("mod_ps"), sem("mod_s"), sem("gate_s")
        var_s, rstd_s, xn_s, xT_ps, hT_s = sem("var_s"), sem("rstd_s"), sem("xn_s"), sem("xT_ps"), sem("hT_s")
        qk_ps, v_ps, q32_s, qk_used, v_s, piece_s = sem("qk_ps"), sem("v_ps"), sem("q32_s"), sem("qk_used"), sem("v_s"), sem("piece_s")
        piece_out = [sem(f"piece_out{c}") for c in range(NC_)]
        aug0_in = [sem(f"aug0_in{c}") for c in range(NC_)]
        aug_in, aug_free, const_in = sem("aug_in"), sem("aug_free"), [sem("const_in0"), sem("const_in1")]
        s1_ready, s1_free = sem("s1_ready"), sem("s1_free")
        tick_s, nmax_s, nmp_s = sem("tick_s"), sem("nmax_s"), sem("nmp_s")
        s2_ready, exp_done = sem("s2_ready"), sem("exp_done")
        rows_s, rows_in = sem("rows_s"), [sem("rows_in0"), sem("rows_in1")]
        pv_done, yT_pe, yT_dve, rl_s, yN_s, yn_s = sem("pv_done"), sem("yT_pe"), sem("yT_dve"), sem("rl_s"), sem("yN_s"), sem("yn_s")
        v_used, v_ready = sem("v_used"), sem("v_ready")
        wp_s, w2_s = sem("wp_s"), sem("w2_s")
        pj_ps, x2_s = sem("pj_ps"), sem("x2_s")
        lraw_s = sem("lraw_s")
        w1_s, hlo_s = sem("w1_s"), sem("hlo_s")
        lg_ps, lg_s, pe_s, d_s, ed_s = sem("lg_ps"), sem("lg_s"), sem("pe_s"), sem("d_s"), sem("ed_s")
        up_ready, hs_ready, y_ready, y_free = (sem(n) for n in ("up_ready", "hs_ready", "y_ready", "y_free"))
        out_s, stored = sem("out_s"), sem("stored")

        x_v = a["x"].rearrange("(n p) c -> p n c", p=P)
        o_v = a["out"].rearrange("(n p) c -> p n c", p=P)
        qa4 = q_aug[:, :].rearrange("r (b h t) -> r b h t", b=2, h=HG)
        ka4 = k_aug[:, :].rearrange("r (b h t) -> r b h t", b=2, h=HG)

        block = ctx.enter_context(nc.Block())

        def load_stack(e, g, buf, c0, c1, done):
            t0, t1 = c0 * CW, c1 * CW
            for i in range(3):
                src = q_dram[i].rearrange("(h d) j t -> h (d j) t", d=D)
                e.dma_start(qa4[PAIR * i:PAIR * (i + 1), ds(buf, 1), :, t0:t1].rearrange("r b h t -> r (b h) t"),
                            src[ds(g * HG, HG), :, t0:t1].rearrange("h r t -> r h t")).then_inc(done, 16)
                src = k_dram.rearrange("(h d) j t -> h (d j) t", d=D)
                e.dma_start(ka4[PAIR * i:PAIR * (i + 1), ds(buf, 1), :, t0:t1].rearrange("r b h t -> r (b h) t"),
                            src[ds(g * HG, HG), :, t0:t1].rearrange("h r t -> r h t")).then_inc(done, 16)

        def load_alibi(e, g, buf, done):
            for k, aug in enumerate((qa4, ka4)):
                e.dma_start(aug[ALIBI0:ALIBI0 + 4, ds(buf, 1), :, :].rearrange("r b h t -> r (b h) t"),
                            a["alibi"][k].rearrange("r h t -> r h t")[:, ds(g * HG, HG), :]).then_inc(done, 16)

        def send_rows(e, u, buf):
            t0 = (u % NC_) * CW
            for i in range(3):
                dst = qa4[MAX0 + i:MAX0 + i + 1, ds(buf, 1), :, t0:t0 + CW]
                e.dma_start(dst.rearrange("r b h t -> r (b h) t"),
                            rows[HG * i:HG * (i + 1), u % 2, :]).then_inc(rows_in[u % 2], 16)

        @block.sync
        def _(sp):
            for c in range(NC_):
                sp.dma_start(x_sb[:, TPC * c:TPC * (c + 1), :], x_v[:, TPC * c:TPC * (c + 1), :]).then_inc(x_in[c], 16)
            def constant_rows(k):
                sp.wait_ge(pad_set, 2 * k + 2)
                load_alibi(sp, k, k, const_in[k])
                sp.dma_start(ka4[MAX0:MAX0 + 3, k, :, :], a["ones3"]).then_inc(const_in[k], 16)

            constant_rows(0)
            for c in range(NC_):
                sp.wait_ge(piece_s, 2 * (c + 1))
                for i in range(3):
                    sp.dma_start(q_dram[i, :, 0:3 - i, c * CW:(c + 1) * CW], pieces[:, c % 2, 0, i:3, :]).then_inc(piece_out[c], 16)
                    if i:
                        sp.dma_start(q_dram[i, :, 3 - i:3, c * CW:(c + 1) * CW], pieces[:, c % 2, 0, 0:i, :]).then_inc(piece_out[c], 16)
                sp.dma_start(k_dram[:, :, c * CW:(c + 1) * CW], pieces[:, c % 2, 1, :, :]).then_inc(piece_out[c], 16)
                sp.wait_ge(piece_out[c], 6 * 16)
                load_stack(sp, 0, 0, c, c + 1, aug0_in[c])

            def group(g, first, last):
                for p in range(-1, NSTEP):
                    if p == 0 and not last:
                        take(sp, aug_free, 1)
                        nxt = g + 1
                        buf = nxt % 2 if first else sp.snap(nxt % 2)
                        load_stack(sp, nxt, buf, 0, NC_, aug_in)
                        if not first:
                            load_alibi(sp, nxt, buf, aug_in)
                    for u in turns(p, first, last):
                        if first and u == 0:
                            continue
                        take(sp, rows_s, 1)
                        gu = g + u // NC_
                        send_rows(sp, u, gu % 2 if isinstance(gu, int) else sp.snap(gu % 2))

            constant_rows(1)
            for dst, src in ((rwT[:, :], a["rwT"]), (tri8[:, :, :], a["tri8"]), (scale_bc[:, :], a["scale"].to_broadcast([P, E]))):
                sp.dma_start(dst, src).then_inc(late_in, 16)
            group(0, True, False)
            with sp.Fori(1, G - 1) as g:
                group(g, False, False)
            take(sp, aug_free, 1)
            for dst, src in ((w1T[:, :], a["w1T"]), (w2T, a["w2T"])):
                sp.dma_start(dst, src).then_inc(late_in, 16)
            group(G - 1, False, True)
            for c in range(NC_):
                sp.wait_ge(out_s, c + 1)
                sp.dma_start(o_v[:, TPC * c:TPC * (c + 1), :], x_sb[:, TPC * c:TPC * (c + 1), :]).then_inc(stored, 16)
            sp.wait_ge(stored, 16 * NC_)

        @block.tensor
        def _(pe):
            mm = nc.tensor.matmul
            pe.wait_ge(wmod_in, 16)
            pe.wait_ge(silu_c, 1)
            for n, m in enumerate((0, 1, 3, 4)):
                last = mm(b1[:, 3, n:n + 1], wmod[:, m * C:(m + 1) * C], sil[:, :], start=True, stop=True)
            last.then_inc(mod_ps, 1)
            pe.wait_ge(w_in, 4 * 16)

            def turn_tokens(c, out, done):
                for i in range(TPC):
                    last = nc.tensor.transpose(out[:, i * P:(i + 1) * P], xn[:, TPC * c + i, :], ident[:, :])
                last.then_inc(done, 1)

            for c in range(NC_):
                pe.wait_ge(xn_s, c + 1)
                if c >= 2:
                    pe.wait_ge(hT_s, c - 1)
                turn_tokens(c, b2[:, c % 2, :], xT_ps)
                pe.wait_ge(hT_s, c + 1)
                for n in range(2):
                    if c:
                        pe.wait_ge(q32_s, 2 * (c - 1) + n + 1)
                    mm(b1[:, n, :], wqkv[:, n * C:(n + 1) * C], hT[:, c * CW:(c + 1) * CW], start=True, stop=True).then_inc(qk_ps, 1)
                if c:
                    pe.wait_ge(v_s, c)
                for i in range(TPC):
                    t = (TPC * c + i) * P
                    last = mm(b1[:, 2, i * C:(i + 1) * C], hT[:, t:t + P], wqkv[:, 2 * C:3 * C], start=True, stop=True)
                last.then_inc(v_ps, 1)
                if c == 0:
                    pe.wait_ge(silbc_s, 1)
                    pe.wait_ge(modc_s, 1)
                    for n, m in enumerate((2, 5)):
                        last = mm(b1[:, 3, n * C:(n + 1) * C], silbc[:, :], wmod[:, m * C:(m + 1) * C], start=True, stop=True)
                    last.then_inc(gate_ps, 1)
            pe.wait_ge(gate_s, 1)
            pe.wait_ge(mask_in, 3 * 16)
            pe.wait_ge(q32_s, 2 * NC_)
            pe.wait_ge(v_s, NC_)
            pe.sem_inc(s1_free, RING1)
            pe.sem_inc(yT_pe, 1)

            def banks(c):
                return (b1[:, 0, :], b1[:, 1, :], b1[:, 2, :]) if c < NC_ - 1 else (pv[:, :], b2[:, 2, :], pv[:, :])

            def project(c):
                pe.wait_ge(yn_s, NC_ * (G - 1) + c + 1)
                pe.wait_ge(wp_s, 1)
                if 0 < c < NC_ - 1:
                    pe.wait_ge(x2_s, c)
                for i in range(TPC):
                    t = (TPC * c + i) * P
                    for g in range(G):
                        last = mm(banks(c)[0][:, i * C:(i + 1) * C], yn[:, g * T + t:g * T + t + P], wproj[:, g, :], start=(g == 0), stop=(g == G - 1))
                last.then_inc(pj_ps, 1)

            def turn_late(c):
                pe.wait_ge(xn_s, NC_ + c + 1)
                if 0 < c < NC_ - 1:
                    pe.wait_ge(hT_s, NC_ + c)
                turn_tokens(c, banks(c)[1], xT_ps)

            def logits(c):
                pe.wait_ge(hT_s, NC_ + c + 1)
                pe.wait_ge(late_in, 5 * 16)
                if 0 < c < NC_ - 1:
                    pe.wait_ge(lraw_s, c)
                for i in range(TPC):
                    t = (TPC * c + i) * P
                    last = mm(banks(c)[2][:, i * E:(i + 1) * E], hT[:, t:t + P], rwT[:, :], start=True, stop=True)
                last.then_inc(lg_ps, 1)

            def group(g, first, last):
                cur = 0 if first else 1 if last else pe.snap(g % 2)
                nxt = 1 if first else None if last else pe.snap(1 - cur)
                n_task = [0]
                at = [0 if first else LEAD]
                freed = []
                n_exp = [0]

                def stack(aug, n, buf, hh, t, w):
                    if isinstance(buf, int):
                        return aug[0:n, buf, hh, t:t + w]
                    return aug[0:n, ds(buf, 1), hh, t:t + w].rearrange("r b t -> r (b t)")

                def pass1(upto):
                    while at[0] < upto:
                        k = at[0]
                        j, c, r, hh = TASKS[k % NTASK]
                        off = cur if k < NTASK else nxt
                        if first and k < NTASK and k == TSTART[j]:
                            pe.wait_ge(aug0_in[j], 6 * 16)
                        if first and k == 0:
                            pe.wait_ge(const_in[0], 3 * 16)
                        if k == NTASK:
                            take(pe, aug_in, (6 if first else 8) * 16)
                            if first:
                                pe.wait_ge(const_in[1], 3 * 16)
                        n_task[0] += 1
                        pe.wait_ge(s1_free, n_task[0])
                        w = (r + 1) * P if c == j else CW
                        mm(b1[:, k % RING1, 0:w], stack(qa4, ROWS1, off, hh, j * CW + r * P, P), stack(ka4, ROWS1, off, hh, c * CW, w),
                           start=True, stop=True).then_inc(s1_ready, 1)
                        at[0] += 1

                def turn(u):
                    take(pe, nmp_s, 1)
                    slot = len(freed) % RING2
                    wait_slot()
                    out = b2[0:3 * HG, slot, 0:CW // 2].bitcast(bf16)
                    for i in range(TPC):
                        last_ = nc.tensor.transpose(out[:, i * P:(i + 1) * P], nmp[:, u % 2, i, :, :], identb[:, :])
                    last_.then_inc(s2_ready, 1)
                    freed.append(None)

                def wait_slot():
                    k = len(freed) - RING2
                    if k >= 0:
                        if freed[k] is None:
                            k += 1
                        pe.wait_ge(*freed[k])

                def step(p):
                    if p == 0:
                        for u in turns(-1, first, last):
                            pass1(TSTART[u + 1] + SETTLE)
                            turn(u)
                    if p < NSTEP:
                        j, kbs = STEPS[p]
                        for hh in range(HG):
                            pass1(min(PLAN[first][p][hh], NTASK) if last else PLAN[first][p][hh])
                            if p == START[j] and hh == 0:
                                take(pe, rows_in[j % 2], 3 * 16)
                            wait_slot()
                            bank, at_ = b2[:, len(freed) % RING2, :], 0
                            for kb in kbs:
                                w, diag = width(j, kb), kb >= TPC * j
                                ins = mm(bank[:, at_:at_ + w], stack(ka4, ROWS2, cur, hh, kb * P, P), stack(qa4, ROWS2, cur, hh, (j + 1) * CW - w, w),
                                         start=True, stop=True)
                                if diag:
                                    ins = mm(bank[:, at_:at_ + P], identb[:, :], maskT[:, :], start=False, stop=True, skip_group_check=True)
                                at_ += w
                            ins.then_inc(s2_ready, 1)
                            n_exp[0] += 1
                            freed.append((exp_done, n_exp[0]))
                        for u in turns(p, first, last):
                            turn(u)
                    if last:
                        if p == min(PROJECT):
                            assert at[0] == NTASK
                            pe.wait_ge(s1_free, n_task[0] + RING1)
                        for way, do in ((PROJECT, project), (TURN, turn_late), (LOGITS, logits)):
                            if p in way:
                                do(way[p])
                    if p >= 1:
                        j, kbs = STEPS[p - 1]
                        pe.wait_ge(exp_done, HG * p)
                        if kbs[0] == 0:
                            take(pe, yT_pe, 1)
                        if kbs[0] == TPC * j:
                            take(pe, v_ready, 1)
                        at_ = 0
                        for kb in kbs:
                            w = width(j, kb)
                            for hh in range(HG):
                                ins = mm(pv[32 * hh:32 * hh + 32, CW - w:CW], v_cur[:, kb, hh, :], probs[:, (p - 1) % 2, hh, at_:at_ + w],
                                         start=(kb == 0), stop=(p == START[j + 1]), skip_group_check=True)
                                if hh == 0 and (p - 1 == 0 or (p - 1 - START[3] in (4, 8, 12))):
                                    ins.then_inc(v_used, 1)
                            at_ += w
                        ins.then_inc(pv_done, 1)

                for p0 in range(0, NSTEP + 1, SECTION):
                    with ExitStack() as part_:
                        if not (first or last):
                            part_.enter_context(pe.Fori(0, 1))
                        for p in range(p0, min(p0 + SECTION, NSTEP + 1)):
                            step(p)
                pe.sem_inc(s1_free, -n_task[0])
                pe.sem_inc(exp_done, -n_exp[0])
            pe.sem_inc(aug_free, 1)
            group(0, True, False)
            pe.sem_inc(aug_free, 1)
            with pe.Fori(1, G - 1) as g:
                group(g, False, False)
                pe.sem_inc(aug_free, 1)
            group(G - 1, False, True)

            pe.wait_ge(late_in, 5 * 16)
            pe.wait_ge(w1_s, E)
            pe.wait_ge(hlo_s, NC_ - 1)
            pe.wait_ge(w2_s, 8)
            pe.wait_ge(lraw_s, NC_ - 1)
            pe.sem_inc(hs_ready, RING1)
            pe.sem_inc(y_free, 2)

            def chunk(t0, first):
                def down(e):
                    pe.wait_ge(hs_ready, RING1 + FC * (e + 1))
                    pe.wait_ge(y_free, e + 1)
                    for i in range(TPC):
                        for f in range(FC):
                            last = mm(b2[:, e % 2, i * C:(i + 1) * C], hs[:, e % 2, f, i * P:(i + 1) * P], w2T[:, e * FC + f, :],
                                      start=(f == 0), stop=(f == FC - 1))
                    last.then_inc(y_ready, 1)

                for e in range(E):
                    if first and e in LAST_WAY:
                        {"project": project, "turn": turn_late, "logits": logits}[LAST_WAY[e]](NC_ - 1)
                    for f in range(FC):
                        n = e * FC + f
                        pe.wait_ge(hs_ready, n + 1)
                        hi, lo = w1_hi[:, n * P:(n + 1) * P], w1_lo[:, n * P:(n + 1) * P]
                        mm(b1[:, n % RING1, :], hi, h_hi[:, ds(t0, CW)], start=True, stop=False)
                        mm(b1[:, n % RING1, :], hi, h_lo[:, ds(t0, CW)], start=False, stop=False)
                        mm(b1[:, n % RING1, :], lo, h_hi[:, ds(t0, CW)], start=False, stop=True).then_inc(up_ready, 1)
                    if e:
                        down(e - 1)
                down(E - 1)
                pe.sem_inc(hs_ready, -E * FC)
                pe.sem_inc(y_free, -E)

            chunk(0, True)
            pe.wait_ge(hlo_s, NC_)
            with pe.Fori(1, NC_) as c:
                chunk(pe.snap(c * CW), False)

        @block.vector
        def _(dve):
            own = Own(dve, dve_s)
            own.inc(nc.vector.memset(ones[:, :], 1.0))
            norms = []

            def statistics(c):
                if c == len(norms):
                    dve.wait_ge(x_in[c], 16)
                n0, n1 = TPC * c, TPC * (c + 1)
                for n in range(n0, n1):
                    own.inc(nc.vector.bn_stats(stats[:, n, :], x_sb[:, n, :]))
                own.wait()
                for n in range(n0, n1):
                    last = nc.vector.bn_aggr(mv[:, n, :], stats[:, n, :])
                last.then_inc(var_s, 1)

            def scale_tokens(c):
                norms.append(c)
                dve.wait_ge(rstd_s, len(norms))
                for n in range(TPC * c, TPC * (c + 1)):
                    last = nc.vector.tensor_scalar(xn[:, n, :], x_sb[:, n, :], mv[:, n, 0:1], rstd[:, n:n + 1], ALU.subtract, ALU.mult)
                last.then_inc(xn_s, 1)

            statistics(0)
            dve.wait_ge(silu_c, 1)
            nc.vector.tensor_scalar(silbc[:, :], ones[:, :], sil[:, 0:1], None, ALU.mult).then_inc(silbc_s, 1)
            scale_tokens(0)
            dve.wait_ge(mod_ps, 1)
            own.inc(nc.vector.tensor_scalar(modc[:, 1:4:2], b1[:, 3, 1:4:2], 1.0, None, ALU.add))
            nc.vector.tensor_copy(modc[:, 0:4:2], b1[:, 3, 0:4:2]).then_inc(modc_s, 1)
            dve.wait_ge(w_in, 4 * 16)
            nc.vector.tensor_scalar(bqk[:, 0:1], bqk[:, 0:1], D ** -0.5, None, ALU.mult).then_inc(bqk_s, 1)
            statistics(1)
            scale_tokens(1)

            def gates():
                dve.wait_ge(gate_ps, 1)
                g_ps = b1[:, 3, 0:2 * C].rearrange("p (a c) -> p a c", a=2)
                own.inc(nc.vector.tensor_scalar(gsgn[:, :, :], g_ps, 0.0, 2.0, ALU.is_ge, ALU.mult))
                own.inc(nc.vector.tensor_scalar(gabs[:, :, :], g_ps, -1.0, None, ALU.mult))
                own.wait()
                own.inc(nc.vector.tensor_tensor(gabs[:, :, :], g_ps, gabs[:, :, :], ALU.max))
                own.wait()
                own.inc(nc.vector.tensor_scalar(gabs[:, :, :], gabs[:, :, :], 0.25, None, ALU.max))
                own.wait()
                nc.vector.scalar_tensor_tensor(gate[:, :, :], gsgn[:, :, :], -1.0, gabs[:, :, :], ALU.add, ALU.mult).then_inc(gate_s, 1)

            for c in range(NC_):
                for n in range(2):
                    dve.wait_ge(q32_s, 2 * c + n + 1)
                    own.inc(nc.vector.tensor_tensor(res[:, n, :], q32[:, n, :], pieces[:, c % 2, n, 0, :], ALU.subtract))
                    own.wait()
                    own.inc(nc.vector.tensor_copy(pieces[:, c % 2, n, 1, :], res[:, n, :]))
                    own.wait()
                    nc.vector.tensor_tensor(pieces[:, c % 2, n, 2, :], res[:, n, :], pieces[:, c % 2, n, 1, :], ALU.subtract).then_inc(piece_s, 1)
                dve.wait_ge(v_ps, c + 1)
                nc.vector.tensor_tensor(v_all[:, TPC * c:TPC * (c + 1), :], b1[:, 2, :].rearrange("p (b c) -> p b c", b=TPC),
                                        bv_bc[:, None, :].to_broadcast([P, TPC, C]), ALU.add).then_inc(v_s, 1)
                if c + 2 < NC_:
                    statistics(c + 2)
                    scale_tokens(c + 2)
                if c == 0:
                    gates()

            def norm_a(j):
                take(dve, yT_dve, 1)
                k = j % 2
                mine.inc(nc.vector.transpose(yB[:, k, :, :].rearrange("p b q -> p (b q)"), yT[:, k, :]))
                mine.wait()
                nc.vector.reciprocal(rl[:, k, :], yB[:, k, :, D]).then_inc(rl_s, 1)

            def norm_b(j):
                take(dve, rB_s, 1)
                k = j % 2
                nc.vector.transpose(yB[:, k, :, :].rearrange("p b q -> p (b q)"), yN[:, k, :, :].rearrange("p b q -> p (b q)")).then_inc(rT_s, 1)

            mine = Own(dve, dve_g)

            def group(first, last):
                n_task, at = 0, 0 if first else LEAD
                for p in range(-1, NSTEP):
                    if p >= 0:
                        for base, j in NORM_AT:
                            if p == base and not (first and j == 3):
                                norm_a(j)
                            if p == base + 2 and not (first and j == 3):
                                norm_b(j)
                    upto = PLAN[first][p][-1] if p >= 0 else 0
                    if last:
                        upto = min(upto, NTASK)
                        for way, do in ((PROJECT, residual), (LOGITS, keep_logits), (ROUTE, lambda part_: route(0, part_))):
                            if p in way:
                                do(way[p])
                    while at < upto:
                        k = at % NTASK
                        j, c, r, hh = TASKS[k]
                        n_task += 1
                        dve.wait_ge(s1_ready, n_task)
                        dst = part[:, j % 2, r * HG + hh, c:c + 1]
                        if c == j:
                            w = (r + 1) * P
                            nc.vector.tensor_tensor_reduce(out=junk[:, k % RING1, 0:w], in0=b1[:, k % RING1, 0:w], in1=mask[:, CW - w:CW],
                                                           scale=1.0, scalar=3 * BIG, op0=ALU.add, op1=ALU.max,
                                                           accum_out=dst).then_inc(s1_free, 1)
                        else:
                            nc.vector.tensor_reduce(dst, b1[:, k % RING1, :], AX.X, ALU.max).then_inc(s1_free, 1)
                        at += 1
                        if k + 1 == TSTART[j + 1]:
                            mine.inc(nc.vector.memset(tick[:, 0:1], 0.0))
                            mine.wait()
                            nc.vector.tensor_reduce(nmax[:, j % 2, :, :].rearrange("p r h -> p (r h)"), part[:, j % 2, :, 0:j + 1], AX.X, ALU.max,
                                                    negate=True).then_inc(nmax_s, 1)
                dve.sem_inc(s1_ready, -n_task)
                mine.reset()

            V = nc.vector

            def step(ins):
                own.inc(ins)
                own.wait()

            def residual(c):
                dve.wait_ge(pj_ps, c + 1)
                xc = x_sb[:, TPC * c:TPC * (c + 1), :]
                o = (pv[:, :] if c == NC_ - 1 else b1[:, 0, :]).rearrange("p (b c) -> p b c", b=TPC)
                V.tensor_tensor(xc, o, xc, ALU.add).then_inc(x2_s, 1)
                dve.wait_ge(x2_s, c + 1)
                statistics(c)
                scale_tokens(c)

            def keep_logits(c):
                dve.wait_ge(lg_ps, c + 1)
                o = (pv if c == NC_ - 1 else b1[:, 2, :])[:, 0:TPC * E].rearrange("p (n e) -> p n e", e=E)
                V.tensor_copy(lraw[:, TPC * c:TPC * (c + 1), :], o).then_inc(lraw_s, 1)
                t = slice(CW * c, CW * (c + 1))
                V.tensor_tensor(h_lo[:, t], hT[:, t], h_hi[:, t].bitcast(fp32), ALU.subtract).then_inc(hlo_s, 1)

            def route(k, part):
                n0, NH = 2 * TPC * k, 2 * TPC
                n = slice(n0, n0 + NH)
                wide = [P, NH, E]
                if part == 0:
                    dve.wait_ge(lraw_s, 2 * (k + 1))
                    step(V.tensor_reduce(lmax[:, n], lraw[:, n, :], AX.X, ALU.max))
                    V.tensor_tensor(lg[:, n, :], lraw[:, n, :], lmax[:, n].unsqueeze(2).to_broadcast(wide), ALU.subtract).then_inc(lg_s, 1)
                if part == 1:
                    dve.wait_ge(pe_s, k + 1)
                    step(V.tensor_reduce(psm[:, n], pr[:, n, :], AX.X, ALU.add))
                    step(V.reciprocal(psm[:, n], psm[:, n]))
                    step(V.tensor_tensor(pr[:, n, :], pr[:, n, :], psm[:, n].unsqueeze(2).to_broadcast(wide), ALU.mult))
                    each = [P, NH, E, E]
                    mine_e = pr[:, n, :].unsqueeze(3).to_broadcast(each)
                    other_e = pr[:, n, :].unsqueeze(2).to_broadcast(each)
                    own.inc(V.tensor_tensor(gt[:, n, :, :], other_e, mine_e, ALU.is_gt))
                    step(V.tensor_tensor(eq[:, n, :, :], other_e, mine_e, ALU.is_equal))
                    step(V.tensor_tensor(eq[:, n, :, :], eq[:, n, :, :], tri8[:, None, :, :].to_broadcast(each), ALU.mult))
                    step(V.tensor_tensor(gt[:, n, :, :], gt[:, n, :, :], eq[:, n, :, :], ALU.add))
                    step(V.tensor_reduce(rank[:, n, :], gt[:, n, :, :], AX.X, ALU.add))
                    for b in range(TOPK):
                        step(V.tensor_scalar(hot[:, b, n, :], rank[:, n, :], float(b), None, ALU.is_equal))
                        step(V.tensor_tensor(lg[:, n, :], hot[:, b, n, :], pr[:, n, :], ALU.mult))
                        step(V.tensor_reduce(ptop[:, b, n], lg[:, n, :], AX.X, ALU.add))
                    V.tensor_tensor(wtop[:, 0, n], ptop[:, 1, n], ptop[:, 0, n], ALU.subtract).then_inc(d_s, 1)
                if part == 2:
                    dve.wait_ge(ed_s, k + 1)
                    step(V.tensor_scalar(psm[:, n], wtop[:, 1, n], 1.0, None, ALU.add))
                    step(V.reciprocal(wtop[:, 0, n], psm[:, n]))
                    step(V.tensor_tensor(wtop[:, 1, n], wtop[:, 1, n], wtop[:, 0, n], ALU.mult))
                    for b in range(TOPK):
                        step(V.tensor_tensor(hot[:, b, n, :], hot[:, b, n, :], wtop[:, b, n].unsqueeze(2).to_broadcast(wide), ALU.mult))
                    step(V.tensor_tensor(comb[:, n, :], hot[:, 0, n, :], hot[:, 1, n, :], ALU.add))
                    step(V.tensor_tensor(comb[:, n, :], comb[:, n, :], scale_bc[:, None, :].to_broadcast(wide), ALU.mult))

            dve.wait_ge(mask_in, 3 * 16)
            group(True, False)
            with dve.Fori(1, G - 1):
                group(False, False)
            group(False, True)
            norm_a(3)
            norm_b(3)
            mine.reset()

            cf = comb[:, :, :].rearrange("p n e -> p (n e)")
            xf = x_sb[:, :, :].rearrange("p n c -> p (n c)")

            def chunk(n0, t0, first):
                for e in range(E):
                    if first and e == 1:
                        residual(NC_ - 1)
                    if first and e == 4:
                        keep_logits(NC_ - 1)
                    dve.wait_ge(y_ready, e + 1)
                    for i in range(TPC):
                        y, w = b2[:, e % 2, i * C:(i + 1) * C], cf[:, ds(n0 + (i * E + e), 1)]
                        if e == 1:
                            last = V.tensor_scalar(accO[:, i, :], y, w, None, ALU.mult)
                        else:
                            acc = accO[:, i, :] if e % 2 else xf[:, ds(t0 + i * C, C)]
                            last = V.scalar_tensor_tensor(acc, y, w, acc, ALU.mult, ALU.add)
                    last.then_inc(y_free, 1)
                    if first and e in (4, 5):
                        route(1, e - 4)
                dve.sem_inc(y_ready, -E)
                mine.inc(V.memset(tick[:, 0:1], 0.0))
                mine.wait()
                V.tensor_tensor(xf[:, ds(t0, CW)], xf[:, ds(t0, CW)], accO[:, :, :].rearrange("p b c -> p (b c)"), ALU.add).then_inc(out_s, 1)
                mine.inc(V.memset(tick[:, 2:3], 0.0))
                mine.reset()

            chunk(0, 0, True)
            route(1, 2)
            with dve.Fori(1, NC_) as c:
                chunk(dve.snap(c * (TPC * E)), dve.snap(c * CW), False)

        @block.scalar
        def _(act):
            for dst, src, done in ((ccol[:, :], a["ccol"], c_in), (wmod[:, :], a["wmod"], wmod_in), (ident[:, :], a["ident"], w_in),
                                   (wqkv[:, :], a["wqkv"], w_in), (bqk[:, :], a["bqk"], w_in),
                                   (bv_bc[:, :], a["bv"].to_broadcast([P, C]), w_in), (mask[:, :], a["mask"], mask_in), (maskT[:, :], a["maskT"], mask_in),
                                   (wproj[:, :, :], a["wproj"], mask_in)):
                act.dma_start(dst, src).then_inc(done, 16)
            act.wait_ge(c_in, 16)
            nc.scalar.activation(sil[:, :], ccol[:, :], ACT.Silu).then_inc(silu_c, 1)
            own = Own(act, act_s)

            def features(c, k):
                act.wait_ge(xT_ps, NC_ * k + c + 1)
                turned_ = b2[:, c % 2, :] if k == 0 else b1[:, 1, :] if c < NC_ - 1 else b2[:, 2, :]
                for dst in (hT, h_hi)[:k + 1]:
                    last = nc.scalar.activation(dst[:, c * CW:(c + 1) * CW], turned_, ACT.Identity,
                                                bias=modc[:, 2 * k:2 * k + 1], scale=modc[:, 2 * k + 1:2 * k + 2])
                last.then_inc(hT_s, 1)

            act.wait_ge(modc_s, 1)
            act.wait_ge(bqk_s, 1)
            for c in range(NC_):
                features(c, 0)
                for n in range(2):
                    act.wait_ge(qk_ps, 2 * c + n + 1)
                    if c:
                        act.wait_ge(piece_s, 2 * (c - 1) + n + 1)
                    if c >= 2 and n == 0:
                        act.wait_ge(piece_out[c - 2], 6 * 16)
                    own.inc(nc.scalar.activation(q32[:, n, :], b1[:, n, :], ACT.Identity, bias=bqk[:, n:n + 1],
                                                 scale=D ** -0.5 if n == 0 else 1.0))
                    own.wait()
                    nc.scalar.activation(pieces[:, c % 2, n, 0, :], q32[:, n, :], ACT.Copy).then_inc(q32_s, 1)

            def route_exp(k, b):
                n = slice(2 * TPC * k, 2 * TPC * (k + 1))
                if b == 0:
                    act.wait_ge(lg_s, k + 1)
                    nc.scalar.activation(pr[:, n, :], lg[:, n, :], ACT.Exp).then_inc(pe_s, 1)
                else:
                    act.wait_ge(d_s, k + 1)
                    nc.scalar.activation(wtop[:, 1, n], wtop[:, 0, n], ACT.Exp).then_inc(ed_s, 1)

            def group(first, last):
                n2 = 0

                def turned(u, n2):
                    act.wait_ge(s2_ready, n2)
                    copy = nc.scalar.activation(rows[:, u % 2, :], b2[0:3 * HG, (n2 - 1) % RING2, 0:CW // 2].bitcast(bf16), ACT.Copy)
                    if first and u == 0:
                        own.inc(copy)
                        own.wait()
                        send_rows(act, 0, 0)
                    else:
                        copy.then_inc(rows_s, 1)

                for u in turns(-1, first, last):
                    n2 += 1
                    turned(u, n2)
                for p in range(NSTEP + 1):
                    if p < NSTEP:
                        w = PASS2[p] // HG
                        if p >= 2:
                            act.wait_ge(pv_done, p - 1)
                        for hh in range(HG):
                            n2 += 1
                            act.wait_ge(s2_ready, n2)
                            nc.scalar.activation(probs[:, p % 2, hh, 0:w], b2[:, (n2 - 1) % RING2, 0:w], ACT.Exp).then_inc(exp_done, 1)
                        for u in turns(p, first, last):
                            n2 += 1
                            turned(u, n2)
                    if last and p in TURN:
                        features(TURN[p], 1)
                    if last and p in ROUTE_EXP:
                        route_exp(0, ROUTE_EXP[p])
                    if p in START[1:]:
                        j = START.index(p) - 1
                        act.wait_ge(pv_done, p)
                        nc.scalar.activation(yT[:, j % 2, :], pv[:, :], ACT.Copy).then_inc(yT_dve, 1)
                        nc.scalar.activation(tick[:, 8 + j:9 + j], ident[:, 0:1], ACT.Copy).then_inc(yT_pe, 1)
                act.sem_inc(s2_ready, -n2)
                act.sem_inc(pv_done, -NSTEP)

            group(True, False)
            with act.Fori(1, G - 1):
                group(False, False)
            group(False, True)

            def chunk(first):
                for n in range(E * FC):
                    e, f = divmod(n, FC)
                    if first and f == 0 and LAST_WAY.get(e) == "turn":
                        features(NC_ - 1, 1)
                    act.wait_ge(up_ready, n + 1)
                    nc.scalar.activation(hs[:, e % 2, f, :], b1[:, n % RING1, :], ACT.Silu).then_inc(hs_ready, 1)
                    if first and n in (7 * FC - 1, E * FC - 1):
                        route_exp(1, int(n == E * FC - 1))
                act.sem_inc(up_ready, -E * FC)

            chunk(True)
            with act.Fori(1, NC_):
                chunk(False)

        @block.gpsimd
        def _(pool):
            own = Own(pool, pool_s)
            u32 = mybir.dt.uint32
            half = HG * T
            def clear_pads(k):
                pool.wait_ge(rstd_s, norms[0])
                own.wait()
                for aug in (q_aug, k_aug):
                    nc.gpsimd.memset(aug[PAD0:ROWS2, k * half:(k + 1) * half].bitcast(u32), 0).then_inc(pad_set, 1)
                pool.wait_ge(pad_set, 2 * k + 2)

            norms = [0]

            def deviation(c):
                norms[0] += 1
                pool.wait_ge(var_s, norms[0])
                n = slice(TPC * c, TPC * (c + 1))
                own.inc(nc.gpsimd.tensor_scalar(rstd[:, n], mv[:, n, 1], EPS, None, ALU.add))
                own.wait()
                nc.gpsimd.tensor_tensor(rstd[:, n], rstd[:, n], neg_half[:, 0:TPC], ALU.pow).then_inc(rstd_s, 1)

            own.inc(nc.gpsimd.memset(neg_half[:, :], -0.5))
            deviation(0)
            clear_pads(0)
            deviation(1)
            own.inc(nc.gpsimd.memset(v_cur[:, :, :, :], 0.0))
            own.wait()
            own.inc(nc.gpsimd.memset(v_cur[:, :, :, D:2 * D], 1.0))
            pool.wait_ge(w_in, 4 * 16)
            own.inc(nc.gpsimd.tensor_copy(identb[:, :], ident[:, :]))
            deviation(2)
            clear_pads(1)
            deviation(3)
            pool.wait_ge(gate_s, 1)
            pool.wait_ge(mask_in, 3 * 16)
            nc.gpsimd.tensor_tensor(wproj[:, :, :], wproj[:, :, :], gate[:, 0:1, :].to_broadcast([P, G, C]), ALU.mult).then_inc(wp_s, 1)
            own.wait()

            def values(q, g):
                b = slice(TPC * q, TPC * (q + 1))
                src = v_all[:, b, ds(g * HG * D, HG * D)].rearrange("p b (h d) -> p b h d", d=D)
                nc.gpsimd.tensor_copy(v_cur[:, b, :, 0:D], src).then_inc(v_ready, 1)

            for q in range(3):
                pool.wait_ge(v_s, q + 1)
                values(q, 0)
            pool.wait_ge(v_s, NC_)
            mine = Own(pool, pool_g)

            def cut_maxima(u):
                take(pool, nmax_s, 1)
                k = u % 2
                mine.inc(nc.gpsimd.tensor_copy(nmp[:, k, :, 0, :], nmax[:, k, :, :]))
                mine.wait()
                mine.inc(nc.gpsimd.tensor_tensor(nres[:, k, :, :], nmax[:, k, :, :], nmp[:, k, :, 0, :], ALU.subtract))
                mine.wait()
                mine.inc(nc.gpsimd.tensor_copy(nmp[:, k, :, 1, :], nres[:, k, :, :]))
                mine.wait()
                nc.gpsimd.tensor_tensor(nmp[:, k, :, 2, :], nres[:, k, :, :], nmp[:, k, :, 1, :], ALU.subtract).then_inc(nmp_s, 1)

            def spread(j):
                take(pool, rl_s, 1)
                k = j % 2
                nc.gpsimd.tensor_copy(yN[:, k, :, :], rl[:, k, :].unsqueeze(2).to_broadcast([P, CW // 32, 32])).then_inc(rB_s, 1)

            def normal(j, g):
                take(pool, rT_s, 1)
                k = j % 2
                nc.gpsimd.tensor_tensor(yn[:, ds(g * T + j * CW, CW)], yT[:, k, :], yB[:, k, :, :].rearrange("p b q -> p (b q)"),
                                        ALU.mult).then_inc(yn_s, 1)

            def group(g, first, last):
                for p in range(-1, NSTEP + 1):
                    for u in turns(p, first, last):
                        cut_maxima(u)
                    if p == 1:
                        take(pool, v_used, 1)
                        values(3, g)
                    if last and p in PROJECT:
                        deviation(PROJECT[p])
                    for base, j in NORM_AT:
                        if not (first and j == 3):
                            if p == base + 1:
                                spread(j)
                            if p == base + 3:
                                normal(j, g - 1 if j == 3 else g)
                    for q in range(3):
                        if p == START[3] + TPC * (q + 1) + 1:
                            take(pool, v_used, 1)
                            if not last:
                                values(q, g + 1)
                    if last and p in W1_AT:
                        e = W1_AT.index(p)
                        if e == 0:
                            pool.wait_ge(late_in, 5 * 16)
                        w = slice(e * F, (e + 1) * F)
                        own.inc(nc.gpsimd.tensor_copy(w1_hi[:, w], w1T[:, w]))
                        own.wait()
                        nc.gpsimd.tensor_tensor(w1_lo[:, w], w1T[:, w], w1_hi[:, w].bitcast(fp32), ALU.subtract).then_inc(w1_s, 1)
                    if last and START[3] + 2 <= p < START[3] + 10:
                        k = p - START[3] - 2
                        if k == 0:
                            pool.wait_ge(late_in, 5 * 16)
                        w = w2T[:, 4 * k:4 * k + 4, :]
                        nc.gpsimd.tensor_tensor(w, w, gate[:, 1:2, :].to_broadcast([P, 4, C]), ALU.mult).then_inc(w2_s, 1)
                mine.reset()

            group(0, True, False)
            with pool.Fori(1, G - 1) as g:
                group(g, False, False)
            group(G - 1, False, True)
            spread(3)
            normal(3, G - 1)
            deviation(NC_ - 1)


def kernel(L0_attn_x, L0_attn_W_attn, L0_attn_b_attn, L0_attn_W_proj, L0_attn_b_proj, L0_ffn_router_w, L0_ffn_w1, L0_ffn_w2,
           L0_ffn_expert_scale, L0_c, L0_wmod):
    import ml_dtypes
    import concourse.bacc as bacc
    from concourse.bass_utils import run_bass_kernel_spmd

    f32 = np.float32
    cont = np.ascontiguousarray
    wproj = np.zeros((HG, 32, G, C), f32)
    wproj[:, 0:D] = np.asarray(L0_attn_W_proj).reshape(G, HG, D, C).transpose(1, 2, 0, 3)
    wproj[0, D, 0] = np.asarray(L0_attn_b_proj)
    slope = (2.0 ** -np.arange(1, H + 1)).astype(f32)[:, None]
    t = np.arange(T)
    one = np.ones((H, T), f32)
    alibi = np.stack([np.stack([-P * slope * (t // P), one, -slope * (t % P), one]),
                      np.stack([one, P * slope * (t // P), one, slope * (t % P)])]).astype(ml_dtypes.bfloat16)
    q, k = np.arange(P)[:, None], np.arange(P)[None, :]
    mask = np.zeros((P, CW), f32)
    mask[:, CW - P:] = np.where(k > q, BIG, 0.0)
    ee = np.arange(E)
    arrays = {
        "x": cont(np.asarray(L0_attn_x).reshape(T, C)),
        "wqkv": cont(L0_attn_W_attn),
        "bqk": cont(np.asarray(L0_attn_b_attn)[:2 * C].reshape(2, C).T),
        "bv": cont(np.asarray(L0_attn_b_attn)[2 * C:].reshape(1, C)),
        "wproj": wproj.reshape(P, G, C),
        "rwT": cont(np.asarray(L0_ffn_router_w).T),
        "w1T": cont(np.asarray(L0_ffn_w1).transpose(2, 0, 1).reshape(C, E * F)),
        "w2T": cont(np.asarray(L0_ffn_w2).reshape(E, C, FC, P).transpose(3, 0, 2, 1).reshape(P, E * FC, C)),
        "scale": cont(np.asarray(L0_ffn_expert_scale).reshape(1, E)),
        "ccol": cont(np.asarray(L0_c).reshape(C, 1)),
        "wmod": cont(L0_wmod),
        "ident": np.eye(P, dtype=f32),
        "mask": mask,
        "maskT": cont(mask[:, CW - P:].T).astype(ml_dtypes.bfloat16),
        "alibi": alibi,
        "ones3": np.ones((3, HG, T), ml_dtypes.bfloat16),
        "tri8": cont(np.broadcast_to((ee[None, :] < ee[:, None]).astype(f32), (P, E, E))),
    }
    nc = bacc.Bacc("TRN2", target_bir_lowering=False, num_devices=1)
    aps = {n: nc.dram_tensor(f"in_{n}", v.shape, mybir.dt.from_np(v.dtype), kind="ExternalInput").ap() for n, v in arrays.items()}
    aps["out"] = nc.dram_tensor("out_0", (T, C), mybir.dt.float32, kind="ExternalOutput").ap()
    build(nc, aps)
    r = run_bass_kernel_spmd(nc, [{f"in_{n}": v for n, v in arrays.items()}], core_ids=[0])
    return np.asarray(r.results[0]["out_0"]).reshape(1, T, C)
```

```python
from contextlib import ExitStack

import numpy as np

import concourse.bass as bass
from concourse import mybir

T, C, H, D = 2048, 128, 16, 8
P = 128
NT = T // P
CW = 512
NC_ = T // CW
TPC = CW // P
HG = 4
G = H // HG
E, F, TOPK = 8, 512, 2
FC = F // P
EPS = 1e-5
BIG = -1e30

PAIR = 3 * D
ALIBI0 = 3 * PAIR
MAX0 = 93
ROWS1, ROWS2 = MAX0, MAX0 + 3
PAD0 = 64

STEPS = [(j, kbs) for j in range(NC_) for kbs in [[kb] for kb in range(TPC * j)] + [[TPC * j], [TPC * j + 1, TPC * j + 3], [TPC * j + 2]]]
NSTEP = len(STEPS)
START = [[s[0] for s in STEPS].index(j) for j in range(NC_)] + [NSTEP]
TASKS = [(j, c, r, hh) for j in range(NC_) for c in range(j + 1) for r in range(TPC) for hh in range(HG)]
TSTART = [TPC * HG * j * (j + 1) // 2 for j in range(NC_ + 1)]
NTASK = len(TASKS)
LEAD = 88
FIRST_LEAD = 14
SETTLE = 7
VALUES_AFTER = {True: 2, False: 3}
SECTION = 4
RING1, RING2 = 4, 3


def width(j, sb):
    return CW - P * max(0, sb - TPC * j)


OVER = 60
PASS2 = [HG * sum(width(j, kb) for kb in kbs) for j, kbs in STEPS]
PASS2_END = [sum(PASS2[:p]) for p in range(NSTEP + 1)]


def task_width(k):
    j, c, r, _ = TASKS[k % NTASK]
    return (r + 1) * P if c == j else CW


def vector_work(k):
    return sum(task_width(i) + OVER for i in range(k))


def plan(first):
    if first:
        knots = [(PASS2_END[START[j]], vector_work(TSTART[j + 1] + SETTLE + (12 if j else FIRST_LEAD))) for j in range(NC_)]
        knots.append((PASS2_END[NSTEP], vector_work(NTASK + LEAD)))
    else:
        knots = [(0, vector_work(LEAD)), (PASS2_END[NSTEP], vector_work(NTASK + LEAD))]
    k, rows_ = 0 if first else LEAD, []
    for p in range(NSTEP):
        row = []
        for hh in range(HG):
            x = PASS2_END[p] + hh * PASS2[p] // HG
            for (x0, y0), (x1, y1) in zip(knots, knots[1:]):
                if x0 <= x <= x1:
                    want = y0 + (y1 - y0) * (x - x0) / (x1 - x0)
            while k < NTASK + LEAD and vector_work(k + 1) <= want:
                k += 1
            if p == NSTEP - 1 and hh == HG - 1:
                k = NTASK + LEAD
            row.append(k)
        rows_.append(row)
    return rows_


PLAN = {first: plan(first) for first in (True, False)}


def turns(p, first, last):
    found = []
    for u in range(2 * NC_ if not last else NC_):
        end = TSTART[u % NC_ + 1] + NTASK * (u // NC_)
        if first and u == 0:
            at = -1
        elif end + SETTLE <= (0 if first else LEAD):
            continue
        else:
            steps = [q for q in range(NSTEP) if PLAN[first][q][-1] >= end + SETTLE]
            if not steps:
                continue
            at = steps[0]
        if at == p:
            found.append(u)
    return found


NORM_AT = ((2, 3), (START[1] + 2, 0), (START[2] + 3, 1), (START[3] + 2, 2))

PROJECT = {19: 0, 21: 1, 27: 2}
TURN = {22: 0, 24: 1, 31: 2}
LOGITS = {24: 0, 25: 1, 32: 2}
HIGH = {23: 0, 24: 1, 31: 2}
ROUTE = {26: 0, 29: 1, 30: 2, 33: 3}
ROUTE_EXP = {27: 0, 32: 1}
W1_AT = [4, 6, 8, 10, 12, 14, 16, 18]
WEIGHTS_AT = NSTEP - 1
LAST_WAY = {2: "project", 3: "turn", 4: "logits"}


def take(e, s, n):
    e.wait_ge(s, n)
    e.sem_inc(s, -n)


class Own:

    def __init__(self, e, s):
        self.e, self.s, self.n = e, s, 0

    def inc(self, ins):
        self.n += 1
        ins.then_inc(self.s, 1)
        return self.n

    def wait(self, n=None):
        self.e.wait_ge(self.s, self.n if n is None else n)

    def reset(self):
        self.wait()
        self.e.sem_inc(self.s, -self.n)
        self.n = 0


def build(nc, a):
    fp32, bf16, fp32r = mybir.dt.float32, mybir.dt.bfloat16, mybir.dt.float32r
    ALU, ACT, AX = mybir.AluOpType, mybir.ActivationFunctionType, mybir.AxisListType
    ds = bass.ds
    with ExitStack() as ctx:
        def sb(name, shape, dt=fp32):
            return ctx.enter_context(nc.sbuf_tensor(name, shape, dt))

        def under(name, shape, dt=fp32):
            with nc.sbuf_tensor(name, shape, dt) as t:
                return t

        def sem(name):
            return ctx.enter_context(nc.semaphore(name))

        x_sb = sb("x_sb", [P, NT, C])
        ident = sb("ident_sb", [P, P])
        mask = sb("mask_sb", [P, CW])
        wqkv = sb("wqkv", [P, 3 * C])
        bqk = sb("bqk", [P, 2])
        bv_bc = sb("bv_bc", [P, C])
        wproj = sb("wproj_sb", [P, G, C])
        ccol = sb("ccol", [P, 1])
        probs = under("probs", [P, 2, HG, CW])
        hs_lo = sb("hs_lo", [P, 2, FC, CW], fp32r)
        early = probs[:, :, :, :].rearrange("p k h t -> p (k h t)")
        wmod = early[:, 0:6 * C]
        rwT = sb("rwT_sb", [P, E])
        scale_bc = sb("scale_bc", [P, E])
        tri8 = sb("tri8_sb", [P, E, E])
        sil = sb("sil", [P, 1])
        ones = early[:, 6 * C:7 * C]
        silbc = early[:, 7 * C:8 * C]
        modc = sb("modc", [P, 4])
        gsgn = early[:, 8 * C:10 * C].rearrange("p (a c) -> p a c", a=2)
        gabs = early[:, 10 * C:12 * C].rearrange("p (a c) -> p a c", a=2)
        gate = sb("gate", [P, 2, C])
        stats = sb("stats", [P, NT, 6])
        mv = sb("mv", [P, NT, 2])
        rstd = sb("rstd", [P, NT])
        nmr = sb("nmr", [P, NT])
        neg_half = sb("neg_half", [P, TPC])
        xn = sb("xn", [P, NT, C])
        hT = under("hT", [P, T])
        h_lo = sb("h_lo", [P, T], fp32r)
        h_hi = sb("h_hi", [P, T], fp32r)
        w1_hi = sb("w1_hi", [P, E * F], fp32r)
        q32 = sb("q32", [P, 2, CW])
        res = sb("res", [P, 2, CW])
        pieces = sb("pieces", [P, 2, 2, 3, CW], bf16)
        v_all = xn
        v_cur = sb("v_cur", [P, NT, HG, 32])
        q_aug = under("q_aug", [P, 2 * HG * T], bf16)
        w1T = under("w1T_sb", [P, E * F])
        w1_lo = sb("w1_lo", [P, E * F], fp32r)
        w2_hi = sb("w2_hi", [P, E * FC, C], fp32r)
        k_aug = under("k_aug", [P, 2 * HG * T], bf16)
        w2T = under("w2T_sb", [P, E * FC, C])
        w2_lo = sb("w2_lo", [P, E * FC, C], fp32r)
        hs_hi = sb("hs_hi", [P, 2, FC, CW], fp32r)
        part = sb("part", [P, 2, TPC * HG, NC_])
        junk = sb("junk", [P, RING1, CW], bf16)
        nmax = sb("nmax", [P, 2, TPC, HG])
        nres = sb("nres", [P, 2, TPC, HG])
        nmp = sb("nmp", [P, 2, TPC, 3, HG], bf16)
        identb = sb("identb", [P, P], bf16)
        maskT = sb("maskT_sb", [P, P], bf16)
        rows = sb("rows", [3 * HG, 2, CW], bf16)
        tick = sb("tick", [P, 32])
        yT = q32
        yB = res[:, :, :].rearrange("p k (b q) -> p k b q", q=32)
        late = pieces[:, :, :, :, :].rearrange("p a b c t -> p (a b c t)").bitcast(fp32)
        yN = late[:, 0:2 * CW].rearrange("p (k b q) -> p k b q", k=2, q=32)
        rl = sb("rl", [P, 2, CW // 32])
        yn = sb("yn", [P, G * T])
        lmax = sb("lmax", [P, NT])
        lraw, lg, pr = (wqkv[:, k * P:(k + 1) * P].rearrange("p (n e) -> p n e", e=E) for k in range(3))
        psm = sb("psm", [P, NT])
        ptop = sb("ptop", [P, 2, NT])
        gt = late[:, 2 * CW:4 * CW].rearrange("p (n e f) -> p n e f", e=E, f=E)
        eq = late[:, 4 * CW:6 * CW].rearrange("p (n e f) -> p n e f", e=E, f=E)
        rank = sb("rank", [P, NT, E])
        hot = sb("hot", [P, 2, NT, E])
        wtop = sb("wtop", [P, 2, NT])
        comb = sb("comb", [P, NT, E])
        hs = probs
        acc = mask
        tmp = junk[:, :, :].rearrange("p a t -> p (a t)").bitcast(fp32)[:, 0:CW]
        combT = sb("combT", [2 * TPC * E, P])
        combB = [yn[:, (e // 2) * T + (e % 2) * CW:(e // 2) * T + (e % 2) * CW + CW] for e in range(E)]

        b1 = ctx.enter_context(nc.psum_tensor("b1", [P, RING1, CW], fp32))
        b2 = ctx.enter_context(nc.psum_tensor("b2", [P, RING2, CW], fp32))
        pv = ctx.enter_context(nc.psum_tensor("pv", [P, CW], fp32))

        q_dram = nc.dram_tensor("q_scratch", (3, P, 3, T), bf16, kind="Internal").ap()
        comb_dram = nc.dram_tensor("comb_scratch", (NT, E, P), fp32, kind="Internal").ap()
        k_dram = nc.dram_tensor("k_scratch", (P, 3, T), bf16, kind="Internal").ap()

        x_in = [sem(f"x_in{c}") for c in range(NC_)]
        c_in, wmod_in, w_in, mask_in, late_in = sem("c_in"), sem("wmod_in"), sem("w_in"), sem("mask_in"), sem("late_in")
        res_s, piece2_s = sem("res_s"), sem("piece2_s")
        modc_s, bqk_s, gate_ps = sem("modc_s"), sem("bqk_s"), sem("gate_ps")
        kpad_set = sem("kpad_set")
        pad_set = [sem("pad_set0"), sem("pad_set1")]
        dve_s, act_s, pool_s = sem("dve_self"), sem("act_self"), sem("pool_self")
        dve_g, pool_g = sem("dve_group"), sem("pool_group")
        rB_s, rT_s = sem("rB_s"), sem("rT_s")
        silu_c, silbc_s, mod_ps, gate_s = sem("silu_c"), sem("silbc_s"), sem("mod_ps"), sem("gate_s")
        var_s, rstd_s, xn_s, xT_ps, hT_s = sem("var_s"), sem("rstd_s"), sem("xn_s"), sem("xT_ps"), sem("hT_s")
        qk_ps, v_ps, q32_s, v_s, piece_s = sem("qk_ps"), sem("v_ps"), sem("q32_s"), sem("v_s"), sem("piece_s")
        piece_out = [sem(f"piece_out{c}") for c in range(NC_)]
        aug0_in = [sem(f"aug0_in{c}") for c in range(NC_)]
        aug_in, aug_free, const_in = sem("aug_in"), sem("aug_free"), [sem("const_in0"), sem("const_in1")]
        s1_ready, s1_free = sem("s1_ready"), sem("s1_free")
        nmax_s, nmp_s = sem("nmax_s"), sem("nmp_s")
        s2_ready, exp_done = sem("s2_ready"), sem("exp_done")
        rows_s, rows_in = sem("rows_s"), [sem("rows_in0"), sem("rows_in1")]
        pv_done, yT_pe, yT_dve, rl_s, yn_s = sem("pv_done"), sem("yT_pe"), sem("yT_dve"), sem("rl_s"), sem("yn_s")
        v_used, v_ready = sem("v_used"), sem("v_ready")
        wp_s, w2_pool = sem("wp_s"), sem("w2_pool")
        pj_ps, x2_s = sem("pj_ps"), sem("x2_s")
        lraw_s = sem("lraw_s")
        w2_dve, lo_s, back_s, acc_s = sem("w2_dve"), sem("lo_s"), sem("back_s"), sem("acc_s")
        ct_ps, ct_s, ct_out, cb_used, comb_s = sem("ct_ps"), sem("ct_s"), sem("ct_out"), sem("cb_used"), sem("comb_s")
        cb_in = [sem(f"cb_in{e}") for e in range(E)]
        hhi_s = sem("hhi_s")
        w1_s, hlo_s = sem("w1_s"), sem("hlo_s")
        lg_ps, lg_s, pe_s, d_s, ed_s = sem("lg_ps"), sem("lg_s"), sem("pe_s"), sem("d_s"), sem("ed_s")
        up_ready, hs_ready, y_ready, y_free = (sem(n) for n in ("up_ready", "hs_ready", "y_ready", "y_free"))
        out_s, stored = sem("out_s"), sem("stored")

        x_v = a["x"].rearrange("(n p) c -> p n c", p=P)
        o_v = a["out"].rearrange("(n p) c -> p n c", p=P)
        qa4 = q_aug[:, :].rearrange("r (b h t) -> r b h t", b=2, h=HG)
        ka4 = k_aug[:, :].rearrange("r (b h t) -> r b h t", b=2, h=HG)

        block = ctx.enter_context(nc.Block())

        def load_stack(e, g, buf, c0, c1, done):
            t0, t1 = c0 * CW, c1 * CW
            for i in range(3):
                src = q_dram[i].rearrange("(h d) j t -> h (d j) t", d=D)
                e.dma_start(qa4[PAIR * i:PAIR * (i + 1), ds(buf, 1), :, t0:t1].rearrange("r b h t -> r (b h) t"),
                            src[ds(g * HG, HG), :, t0:t1].rearrange("h r t -> r h t")).then_inc(done, 16)
                src = k_dram.rearrange("(h d) j t -> h (d j) t", d=D)
                e.dma_start(ka4[PAIR * i:PAIR * (i + 1), ds(buf, 1), :, t0:t1].rearrange("r b h t -> r (b h) t"),
                            src[ds(g * HG, HG), :, t0:t1].rearrange("h r t -> r h t")).then_inc(done, 16)

        def load_alibi(e, g, buf, done):
            for k, aug in enumerate((qa4, ka4)):
                e.dma_start(aug[ALIBI0:ALIBI0 + 4, ds(buf, 1), :, :].rearrange("r b h t -> r (b h) t"),
                            a["alibi"][k].rearrange("r h t -> r h t")[:, ds(g * HG, HG), :]).then_inc(done, 16)

        def send_rows(e, u, buf):
            t0 = (u % NC_) * CW
            for i in range(3):
                dst = qa4[MAX0 + i:MAX0 + i + 1, ds(buf, 1), :, t0:t0 + CW]
                e.dma_start(dst.rearrange("r b h t -> r (b h) t"),
                            rows[HG * i:HG * (i + 1), u % 2, :]).then_inc(rows_in[u % 2], 16)

        @block.sync
        def _(sp):
            loads = [(x_sb[:, TPC * c:TPC * (c + 1), :], x_v[:, TPC * c:TPC * (c + 1), :], x_in[c]) for c in range(NC_)]
            loads[1:1] = [(ident[:, :], a["ident"], w_in), (wqkv[:, :], a["wqkv"], w_in), (bqk[:, :], a["bqk"], w_in),
                          (bv_bc[:, :], a["bv"].to_broadcast([P, C]), w_in)]
            loads += [(mask[:, :], a["mask"], mask_in), (maskT[:, :], a["maskT"], mask_in), (wproj[:, :, :], a["wproj"], mask_in)]
            for dst, src, done in loads:
                sp.dma_start(dst, src).then_inc(done, 16)
            def constant_rows(k):
                sp.wait_ge(pad_set[k], k + 1)
                sp.wait_ge(kpad_set, 1)
                load_alibi(sp, k, k, const_in[k])
                sp.dma_start(ka4[MAX0:MAX0 + 3, k, :, :], a["ones3"]).then_inc(const_in[k], 16)

            constant_rows(0)
            for c in range(NC_ + 1):
                if c < NC_:
                    sp.wait_ge(piece_s, 2 * (c + 1))
                    for i in range(3):
                        sp.dma_start(q_dram[i, :, 0:3 - i, c * CW:(c + 1) * CW], pieces[:, c % 2, 0, i:3, :]).then_inc(piece_out[c], 16)
                        if i:
                            sp.dma_start(q_dram[i, :, 3 - i:3, c * CW:(c + 1) * CW], pieces[:, c % 2, 0, 0:i, :]).then_inc(piece_out[c], 16)
                    sp.dma_start(k_dram[:, :, c * CW:(c + 1) * CW], pieces[:, c % 2, 1, :, :]).then_inc(piece_out[c], 16)
                if c:
                    sp.wait_ge(piece_out[c - 1], 6 * 16)
                    load_stack(sp, 0, 0, c - 1, c, aug0_in[c - 1])

            def group(g, first, last):
                for p in range(-1, NSTEP):
                    if p == 0 and not last:
                        take(sp, aug_free, 1)
                        nxt = g + 1
                        buf = nxt % 2 if first else sp.snap(nxt % 2)
                        load_stack(sp, nxt, buf, 0, NC_, aug_in)
                        if not first:
                            load_alibi(sp, nxt, buf, aug_in)
                    for u in turns(p, first, last):
                        if first and u == 0:
                            continue
                        take(sp, rows_s, 1)
                        gu = g + u // NC_
                        send_rows(sp, u, gu % 2 if isinstance(gu, int) else sp.snap(gu % 2))

            constant_rows(1)
            for dst, src in ((rwT[:, :], a["rwT"]), (tri8[:, :, :], a["tri8"]), (scale_bc[:, :], a["scale"].to_broadcast([P, E]))):
                sp.dma_start(dst, src).then_inc(late_in, 16)
            group(0, True, False)
            with sp.Fori(1, G - 1) as g:
                group(g, False, False)
            take(sp, aug_free, 1)
            for dst, src in ((w1T[:, :], a["w1T"]), (w2T[:, :, :], a["w2T"])):
                sp.dma_start(dst, src).then_inc(late_in, 16)
            group(G - 1, False, True)

            def store_weights(k):
                sp.wait_ge(ct_s, k + 1)
                n = slice(2 * TPC * k, 2 * TPC * (k + 1))
                sp.dma_start(comb_dram[n, :, :].rearrange("n e p -> (n e) p"), combT[:, :]).then_inc(ct_out, 16)
                sp.wait_ge(ct_out, 16 * (k + 1))

            def load_weights(c, first):
                for e in range(E):
                    if not first:
                        take(sp, cb_used, 1)
                    src = comb_dram[ds(c * TPC, TPC), e, :].unsqueeze(0).to_broadcast([P, TPC, P])
                    sp.dma_start(combB[e].rearrange("p (n t) -> p n t", n=TPC), src).then_inc(cb_in[e], 16)

            def store_output(c):
                take(sp, out_s, 1)
                sp.dma_start(o_v[:, ds(c * TPC, TPC), :], x_sb[:, ds(c * TPC, TPC), :]).then_inc(stored, 16)

            store_weights(0)
            load_weights(0, True)
            load_weights(1, False)
            store_output(0)
            store_weights(1)
            with sp.Fori(2, NC_) as c:
                load_weights(c, False)
                store_output(c - 1)
            store_output(NC_ - 1)
            sp.wait_ge(stored, 16 * NC_)

        @block.tensor
        def _(pe):
            mm = nc.tensor.matmul
            pe.wait_ge(wmod_in, 16)
            pe.wait_ge(silu_c, 1)
            for n, m in enumerate((0, 1, 3, 4)):
                last = mm(b1[:, 3, n:n + 1], wmod[:, m * C:(m + 1) * C], sil[:, :], start=True, stop=True)
            last.then_inc(mod_ps, 1)
            pe.wait_ge(w_in, 4 * 16)

            def turn_tokens(c, out, done):
                for i in range(TPC):
                    last = nc.tensor.transpose(out[:, i * P:(i + 1) * P], xn[:, TPC * c + i, :], ident[:, :])
                last.then_inc(done, 1)

            def turn_early(c):
                pe.wait_ge(xn_s, c + 1)
                if c >= 2:
                    pe.wait_ge(hT_s, c - 1)
                turn_tokens(c, b2[:, c % 2, :], xT_ps)

            turn_early(0)
            for c in range(NC_):
                pe.wait_ge(hT_s, c + 1)
                for n in range(2):
                    if c:
                        pe.wait_ge(q32_s, 2 * (c - 1) + n + 1)
                    mm(b1[:, n, :], wqkv[:, n * C:(n + 1) * C], hT[:, c * CW:(c + 1) * CW], start=True, stop=True).then_inc(qk_ps, 1)
                if c + 1 < NC_:
                    turn_early(c + 1)
                if c:
                    pe.wait_ge(v_s, c)
                for i in range(TPC):
                    t = (TPC * c + i) * P
                    last = mm(b1[:, 2, i * C:(i + 1) * C], hT[:, t:t + P], wqkv[:, 2 * C:3 * C], start=True, stop=True)
                last.then_inc(v_ps, 1)
                if c == 0:
                    pe.wait_ge(silbc_s, 1)
                    pe.wait_ge(modc_s, 1)
                    for n, m in enumerate((2, 5)):
                        last = mm(b1[:, 3, n * C:(n + 1) * C], silbc[:, :], wmod[:, m * C:(m + 1) * C], start=True, stop=True)
                    last.then_inc(gate_ps, 1)
            pe.wait_ge(gate_s, 1)
            pe.wait_ge(mask_in, 3 * 16)
            pe.sem_inc(yT_pe, 1)

            def banks(c):
                return (b1[:, 0, :], b1[:, 1, :], b1[:, 2, :]) if c < NC_ - 1 else (pv[:, :], b2[:, 2, :], pv[:, :])

            def project(c, i):
                if i == 0:
                    pe.wait_ge(yn_s, NC_ * (G - 1) + c + 1)
                    pe.wait_ge(wp_s, 1)
                    if 0 < c < NC_ - 1:
                        pe.wait_ge(x2_s, c)
                t = (TPC * c + i) * P
                for g in range(G):
                    last = mm(banks(c)[0][:, i * C:(i + 1) * C], yn[:, g * T + t:g * T + t + P], wproj[:, g, :], start=(g == 0), stop=(g == G - 1))
                if i == TPC - 1:
                    last.then_inc(pj_ps, 1)

            def turn_late(c):
                pe.wait_ge(xn_s, NC_ + c + 1)
                if 0 < c < NC_ - 1:
                    pe.wait_ge(hT_s, NC_ + c)
                turn_tokens(c, banks(c)[1], xT_ps)

            def logits(c):
                pe.wait_ge(hT_s, NC_ + c + 1)
                pe.wait_ge(late_in, 5 * 16)
                if 0 < c < NC_ - 1:
                    pe.wait_ge(lraw_s, c)
                for i in range(TPC):
                    t = (TPC * c + i) * P
                    last = mm(banks(c)[2][:, i * E:(i + 1) * E], hT[:, t:t + P], rwT[:, :], start=True, stop=True)
                last.then_inc(lg_ps, 1)

            def turn_weights(k):
                pe.wait_ge(comb_s, k + 1)
                out = b1[:, 3, :] if k == 0 else pv[:, :]
                nc.tensor.transpose(out[0:2 * TPC * E, 0:P], comb[:, 2 * TPC * k:2 * TPC * (k + 1), :], ident[:, :]).then_inc(ct_ps, 1)

            def group(g, first, last):
                cur = 0 if first else 1 if last else pe.snap(g % 2)
                nxt = 1 if first else None if last else pe.snap(1 - cur)
                n_task = [0]
                at = [0 if first else LEAD]
                freed = []
                n_exp = [0]

                def stack(aug, n, buf, hh, t, w):
                    if isinstance(buf, int):
                        return aug[0:n, buf, hh, t:t + w]
                    return aug[0:n, ds(buf, 1), hh, t:t + w].rearrange("r b t -> r (b t)")

                def pass1(upto):
                    while at[0] < upto:
                        k = at[0]
                        j, c, r, hh = TASKS[k % NTASK]
                        off = cur if k < NTASK else nxt
                        if first and k < NTASK and k == TSTART[j]:
                            pe.wait_ge(aug0_in[j], 6 * 16)
                        if first and k == 0:
                            pe.wait_ge(const_in[0], 3 * 16)
                        if k == NTASK:
                            take(pe, aug_in, (6 if first else 8) * 16)
                            if first:
                                pe.wait_ge(const_in[1], 3 * 16)
                        n_task[0] += 1
                        pe.wait_ge(s1_free, n_task[0])
                        w = (r + 1) * P if c == j else CW
                        mm(b1[:, k % RING1, 0:w], stack(qa4, ROWS1, off, hh, j * CW + r * P, P), stack(ka4, ROWS1, off, hh, c * CW, w),
                           start=True, stop=True).then_inc(s1_ready, 1)
                        at[0] += 1

                def turn(u):
                    take(pe, nmp_s, 1)
                    slot = len(freed) % RING2
                    wait_slot()
                    out = b2[0:3 * HG, slot, 0:CW // 2].bitcast(bf16)
                    for i in range(TPC):
                        last_ = nc.tensor.transpose(out[:, i * P:(i + 1) * P], nmp[:, u % 2, i, :, :], identb[:, :])
                    last_.then_inc(s2_ready, 1)
                    freed.append(None)

                def wait_slot():
                    k = len(freed) - RING2
                    if k >= 0:
                        if freed[k] is None:
                            k += 1
                        pe.wait_ge(*freed[k])

                def value_products(p):
                    j, kbs = STEPS[p - 1]
                    pe.wait_ge(exp_done, HG * p)
                    if kbs[0] == 0:
                        take(pe, yT_pe, 1)
                    if kbs[0] == TPC * j:
                        take(pe, v_ready, 1)
                    at_ = 0
                    for kb in kbs:
                        w = width(j, kb)
                        for hh in range(HG):
                            ins = mm(pv[32 * hh:32 * hh + 32, CW - w:CW], v_cur[:, kb, hh, :], probs[:, (p - 1) % 2, hh, at_:at_ + w],
                                     start=(kb == 0), stop=(p == START[j + 1]), skip_group_check=True)
                            if hh == 0 and (p - 1 == 0 or (p - 1 - START[3] in (4, 8, 12))):
                                ins.then_inc(v_used, 1)
                        at_ += w
                    ins.then_inc(pv_done, 1)

                def step(p):
                    if p == 0:
                        for u in turns(-1, first, last):
                            pass1(TSTART[u + 1] + SETTLE)
                            turn(u)
                    if p < NSTEP:
                        j, kbs = STEPS[p]
                        for hh in range(HG):
                            pass1(min(PLAN[first][p][hh], NTASK) if last else PLAN[first][p][hh])
                            if p == START[j] and hh == 0:
                                take(pe, rows_in[j % 2], 3 * 16)
                            wait_slot()
                            bank, at_ = b2[:, len(freed) % RING2, :], 0
                            for kb in kbs:
                                w, diag = width(j, kb), kb >= TPC * j
                                ins = mm(bank[:, at_:at_ + w], stack(ka4, ROWS2, cur, hh, kb * P, P), stack(qa4, ROWS2, cur, hh, (j + 1) * CW - w, w),
                                         start=True, stop=True)
                                if diag:
                                    ins = mm(bank[:, at_:at_ + P], identb[:, :], maskT[:, :], start=False, stop=True, skip_group_check=True)
                                at_ += w
                            ins.then_inc(s2_ready, 1)
                            n_exp[0] += 1
                            freed.append((exp_done, n_exp[0]))
                            if last and p in PROJECT:
                                if p == min(PROJECT) and hh == 0:
                                    assert at[0] == NTASK
                                    pe.wait_ge(s1_free, n_task[0] + RING1)
                                project(PROJECT[p], hh)
                            if p >= 1 and hh == VALUES_AFTER[last]:
                                value_products(p)
                        for u in turns(p, first, last):
                            turn(u)
                    if last:
                        for way, do in ((TURN, turn_late), (LOGITS, logits)):
                            if p in way:
                                do(way[p])
                        if p == WEIGHTS_AT:
                            turn_weights(0)
                    if p == NSTEP:
                        value_products(p)

                for p0 in range(0, NSTEP + 1, SECTION):
                    with ExitStack() as part_:
                        if not (first or last):
                            part_.enter_context(pe.Fori(0, 1))
                        for p in range(p0, min(p0 + SECTION, NSTEP + 1)):
                            step(p)
                pe.sem_inc(s1_free, -n_task[0])
                pe.sem_inc(exp_done, -n_exp[0])
            pe.sem_inc(aug_free, 1)
            group(0, True, False)
            pe.sem_inc(aug_free, 1)
            with pe.Fori(1, G - 1) as g:
                group(g, False, False)
                pe.sem_inc(aug_free, 1)
            group(G - 1, False, True)

            pe.wait_ge(late_in, 5 * 16)
            pe.wait_ge(w1_s, E)
            pe.wait_ge(hlo_s, NC_ - 1)
            pe.wait_ge(lraw_s, NC_ - 1)
            pe.sem_inc(lo_s, RING1)
            pe.sem_inc(y_free, 2)

            def turn_back():
                take(pe, acc_s, 1)
                for i in range(TPC):
                    last = nc.tensor.transpose(b2[:, 2, i * P:(i + 1) * P], acc[:, i * P:(i + 1) * P], ident[:, :])
                last.then_inc(back_s, 1)

            def chunk(t0, number):
                def down(e):
                    pe.wait_ge(lo_s, RING1 + FC * (e + 1))
                    pe.wait_ge(y_free, e + 1)
                    if number == 0:
                        if e < 2:
                            pe.wait_ge(w2_dve, e + 1)
                        else:
                            pe.wait_ge(w2_pool, e - 1)
                    for f in range(FC):
                        n = e * FC + f
                        for k, (w, h) in enumerate(((w2_hi, hs_hi), (w2_hi, hs_lo), (w2_lo, hs_hi))):
                            last = mm(b2[:, e % 2, :], w[:, n, :], h[:, e % 2, f, :], start=(f == 0 and k == 0), stop=(f == FC - 1 and k == 2))
                    last.then_inc(y_ready, 1)

                for e in range(E):
                    if number == 0 and e in LAST_WAY:
                        {"project": lambda c: [project(c, i) for i in range(TPC)], "turn": turn_late, "logits": logits}[LAST_WAY[e]](NC_ - 1)
                    for f in range(FC):
                        n = e * FC + f
                        pe.wait_ge(lo_s, n + 1)
                        hi, lo = w1_hi[:, n * P:(n + 1) * P], w1_lo[:, n * P:(n + 1) * P]
                        mm(b1[:, n % RING1, :], hi, h_hi[:, ds(t0, CW)], start=True, stop=False)
                        mm(b1[:, n % RING1, :], hi, h_lo[:, ds(t0, CW)], start=False, stop=False)
                        mm(b1[:, n % RING1, :], lo, h_hi[:, ds(t0, CW)], start=False, stop=True).then_inc(up_ready, 1)
                    if e:
                        down(e - 1)
                    elif number != 0:
                        turn_back()
                down(E - 1)
                pe.sem_inc(lo_s, -E * FC)
                pe.sem_inc(y_free, -E)

            pe.wait_ge(ct_s, 1)
            chunk(0, 0)
            pe.wait_ge(hlo_s, NC_)
            chunk(CW, 1)
            turn_weights(1)
            with pe.Fori(2, NC_) as c:
                chunk(pe.snap(c * CW), None)
            turn_back()

        @block.vector
        def _(dve):
            own = Own(dve, dve_s)
            own.inc(nc.vector.memset(ones[:, :], 1.0))

            def statistics(c, setup=False):
                if setup:
                    dve.wait_ge(x_in[c], 16)
                n0, n1 = TPC * c, TPC * (c + 1)
                for n in range(n0, n1):
                    own.inc(nc.vector.bn_stats(stats[:, n, :], x_sb[:, n, :]))
                own.wait()
                for n in range(n0, n1):
                    last = nc.vector.bn_aggr(mv[:, n, :], stats[:, n, :])
                last.then_inc(var_s, 1)

            def scale_tokens(c):
                dve.wait_ge(rstd_s, NC_ + c + 1)
                for n in range(TPC * c, TPC * (c + 1)):
                    last = nc.vector.tensor_scalar(xn[:, n, :], x_sb[:, n, :], mv[:, n, 0:1], rstd[:, n:n + 1], ALU.subtract, ALU.mult)
                last.then_inc(xn_s, 1)

            statistics(0, True)
            statistics(1, True)
            dve.wait_ge(silu_c, 1)
            nc.vector.tensor_scalar(silbc[:, :], ones[:, :], sil[:, 0:1], None, ALU.mult).then_inc(silbc_s, 1)
            dve.wait_ge(mod_ps, 1)
            own.inc(nc.vector.tensor_scalar(modc[:, 1:4:2], b1[:, 3, 1:4:2], 1.0, None, ALU.add))
            nc.vector.tensor_copy(modc[:, 0:4:2], b1[:, 3, 0:4:2]).then_inc(modc_s, 1)
            dve.wait_ge(w_in, 4 * 16)
            nc.vector.tensor_scalar(bqk[:, 0:1], bqk[:, 0:1], D ** -0.5, None, ALU.mult).then_inc(bqk_s, 1)
            nc.vector.memset(k_aug[PAD0:ROWS2, 0:HG * T].bitcast(mybir.dt.uint32), 0).then_inc(kpad_set, 1)
            statistics(2, True)
            statistics(3, True)

            def biased_values(c):
                dve.wait_ge(v_ps, c + 1)
                nc.vector.tensor_tensor(v_all[:, TPC * c:TPC * (c + 1), :], b1[:, 2, :].rearrange("p (b c) -> p b c", b=TPC),
                                        bv_bc[:, None, :].to_broadcast([P, TPC, C]), ALU.add).then_inc(v_s, 1)

            def gates():
                dve.wait_ge(gate_ps, 1)
                g_ps = b1[:, 3, 0:2 * C].rearrange("p (a c) -> p a c", a=2)
                own.inc(nc.vector.tensor_scalar(gsgn[:, :, :], g_ps, 0.0, 2.0, ALU.is_ge, ALU.mult))
                own.inc(nc.vector.tensor_scalar(gabs[:, :, :], g_ps, -1.0, None, ALU.mult))
                own.wait()
                own.inc(nc.vector.tensor_tensor(gabs[:, :, :], g_ps, gabs[:, :, :], ALU.max))
                own.wait()
                own.inc(nc.vector.tensor_scalar(gabs[:, :, :], gabs[:, :, :], 0.25, None, ALU.max))
                own.wait()
                nc.vector.scalar_tensor_tensor(gate[:, :, :], gsgn[:, :, :], -1.0, gabs[:, :, :], ALU.add, ALU.mult).then_inc(gate_s, 1)

            for c in range(NC_):
                for n in range(2):
                    dve.wait_ge(q32_s, 2 * c + n + 1)
                    nc.vector.tensor_tensor(res[:, n, :], q32[:, n, :], pieces[:, c % 2, n, 0, :], ALU.subtract).then_inc(res_s, 1)
                    if c == NC_ - 1:
                        dve.sem_inc(s1_free, 1)
                if c == NC_ - 1:
                    biased_values(c)
                for n in range(2):
                    dve.wait_ge(piece2_s, 2 * c + n + 1)
                    nc.vector.tensor_tensor(pieces[:, c % 2, n, 2, :], res[:, n, :], pieces[:, c % 2, n, 1, :], ALU.subtract).then_inc(piece_s, 1)
                if c < NC_ - 1:
                    biased_values(c)
                if c == 0:
                    gates()
            dve.wait_ge(v_s, NC_)
            dve.sem_inc(s1_free, RING1 - 2)

            def norm_a(j):
                take(dve, yT_dve, 1)
                k = j % 2
                mine.inc(nc.vector.transpose(yB[:, k, :, :].rearrange("p b q -> p (b q)"), yT[:, k, :]))
                mine.wait()
                nc.vector.reciprocal(rl[:, k, :], yB[:, k, :, D]).then_inc(rl_s, 1)

            def norm_b(j):
                take(dve, rB_s, 1)
                k = j % 2
                nc.vector.transpose(yB[:, k, :, :].rearrange("p b q -> p (b q)"), yN[:, k, :, :].rearrange("p b q -> p (b q)")).then_inc(rT_s, 1)

            mine = Own(dve, dve_g)

            def group(first, last):
                n_task, at = 0, 0 if first else LEAD
                for p in range(-1, NSTEP):
                    if p >= 0:
                        for base, j in NORM_AT:
                            if p == base and not (first and j == 3):
                                norm_a(j)
                            if p == base + 2 and not (first and j == 3):
                                norm_b(j)
                    upto = PLAN[first][p][-1] if p >= 0 else 0
                    if last:
                        upto = min(upto, NTASK)
                        for way, do in ((PROJECT, residual), (LOGITS, keep_logits), (ROUTE, lambda part_: route(0, part_))):
                            if p in way:
                                do(way[p])
                        if p == WEIGHTS_AT:
                            keep_weights(0)
                    while at < upto:
                        k = at % NTASK
                        j, c, r, hh = TASKS[k]
                        n_task += 1
                        dve.wait_ge(s1_ready, n_task)
                        dst = part[:, j % 2, r * HG + hh, c:c + 1]
                        if c == j:
                            w = (r + 1) * P
                            nc.vector.tensor_tensor_reduce(out=junk[:, k % RING1, 0:w], in0=b1[:, k % RING1, 0:w], in1=mask[:, CW - w:CW],
                                                           scale=1.0, scalar=3 * BIG, op0=ALU.add, op1=ALU.max,
                                                           accum_out=dst).then_inc(s1_free, 1)
                        else:
                            nc.vector.tensor_reduce(dst, b1[:, k % RING1, :], AX.X, ALU.max).then_inc(s1_free, 1)
                        at += 1
                        if k + 1 == TSTART[j + 1]:
                            mine.inc(nc.vector.memset(tick[:, 0:1], 0.0))
                            mine.wait()
                            nc.vector.tensor_reduce(nmax[:, j % 2, :, :].rearrange("p r h -> p (r h)"), part[:, j % 2, :, 0:j + 1], AX.X, ALU.max,
                                                    negate=True).then_inc(nmax_s, 1)
                dve.sem_inc(s1_ready, -n_task)
                mine.reset()

            V = nc.vector

            def step(ins):
                own.inc(ins)
                own.wait()

            def residual(c):
                dve.wait_ge(pj_ps, c + 1)
                xc = x_sb[:, TPC * c:TPC * (c + 1), :]
                o = (pv[:, :] if c == NC_ - 1 else b1[:, 0, :]).rearrange("p (b c) -> p b c", b=TPC)
                V.tensor_tensor(xc, o, xc, ALU.add).then_inc(x2_s, 1)
                dve.wait_ge(x2_s, c + 1)
                statistics(c)
                scale_tokens(c)

            def keep_logits(c):
                dve.wait_ge(lg_ps, c + 1)
                o = (pv if c == NC_ - 1 else b1[:, 2, :])[:, 0:TPC * E].rearrange("p (n e) -> p n e", e=E)
                V.tensor_copy(lraw[:, TPC * c:TPC * (c + 1), :], o).then_inc(lraw_s, 1)
                if c < NC_ - 1:
                    dve.wait_ge(hhi_s, c + 1)
                t = slice(CW * c, CW * (c + 1))
                V.tensor_tensor(h_lo[:, t], hT[:, t], h_hi[:, t].bitcast(fp32), ALU.subtract).then_inc(hlo_s, 1)

            def route(k, part):
                n0, NH = 2 * TPC * k, 2 * TPC
                n = slice(n0, n0 + NH)
                wide = [P, NH, E]
                if part == 0:
                    dve.wait_ge(lraw_s, 2 * (k + 1))
                    step(V.tensor_reduce(lmax[:, n], lraw[:, n, :], AX.X, ALU.max))
                    V.tensor_tensor(lg[:, n, :], lraw[:, n, :], lmax[:, n].unsqueeze(2).to_broadcast(wide), ALU.subtract).then_inc(lg_s, 1)
                if part == 1:
                    dve.wait_ge(pe_s, k + 1)
                    step(V.tensor_reduce(psm[:, n], pr[:, n, :], AX.X, ALU.add))
                    step(V.reciprocal(psm[:, n], psm[:, n]))
                    step(V.tensor_tensor(pr[:, n, :], pr[:, n, :], psm[:, n].unsqueeze(2).to_broadcast(wide), ALU.mult))
                    each = [P, NH, E, E]
                    mine_e = pr[:, n, :].unsqueeze(3).to_broadcast(each)
                    other_e = pr[:, n, :].unsqueeze(2).to_broadcast(each)
                    own.inc(V.tensor_tensor(gt[:, n, :, :], other_e, mine_e, ALU.is_gt))
                    step(V.tensor_tensor(eq[:, n, :, :], other_e, mine_e, ALU.is_equal))
                if part == 2:
                    each = [P, NH, E, E]
                    step(V.tensor_tensor(eq[:, n, :, :], eq[:, n, :, :], tri8[:, None, :, :].to_broadcast(each), ALU.mult))
                    step(V.tensor_tensor(gt[:, n, :, :], gt[:, n, :, :], eq[:, n, :, :], ALU.add))
                    step(V.tensor_reduce(rank[:, n, :], gt[:, n, :, :], AX.X, ALU.add))
                    for b in range(TOPK):
                        step(V.tensor_scalar(hot[:, b, n, :], rank[:, n, :], float(b), None, ALU.is_equal))
                        step(V.tensor_tensor(lg[:, n, :], hot[:, b, n, :], pr[:, n, :], ALU.mult))
                        step(V.tensor_reduce(ptop[:, b, n], lg[:, n, :], AX.X, ALU.add))
                    V.tensor_tensor(wtop[:, 0, n], ptop[:, 1, n], ptop[:, 0, n], ALU.subtract).then_inc(d_s, 1)
                if part == 3:
                    dve.wait_ge(ed_s, k + 1)
                    step(V.tensor_scalar(psm[:, n], wtop[:, 1, n], 1.0, None, ALU.add))
                    step(V.reciprocal(wtop[:, 0, n], psm[:, n]))
                    step(V.tensor_tensor(wtop[:, 1, n], wtop[:, 1, n], wtop[:, 0, n], ALU.mult))
                    for b in range(TOPK):
                        step(V.tensor_tensor(hot[:, b, n, :], hot[:, b, n, :], wtop[:, b, n].unsqueeze(2).to_broadcast(wide), ALU.mult))
                    step(V.tensor_tensor(comb[:, n, :], hot[:, 0, n, :], hot[:, 1, n, :], ALU.add))
                    V.tensor_tensor(comb[:, n, :], comb[:, n, :], scale_bc[:, None, :].to_broadcast(wide), ALU.mult).then_inc(comb_s, 1)

            def keep_weights(k):
                dve.wait_ge(ct_ps, k + 1)
                V.tensor_copy(combT[:, :], (b1[:, 3, :] if k == 0 else pv[:, :])[0:2 * TPC * E, 0:P]).then_inc(ct_s, 1)

            dve.wait_ge(mask_in, 3 * 16)
            group(True, False)
            with dve.Fori(1, G - 1):
                group(False, False)
            group(False, True)

            def split_w2(e):
                n = slice(e * FC, (e + 1) * FC)
                own.inc(V.tensor_copy(w2_hi[:, n, :], w2T[:, n, :]))
                own.wait()
                V.tensor_tensor(w2_lo[:, n, :], w2T[:, n, :], w2_hi[:, n, :].bitcast(fp32), ALU.subtract).then_inc(w2_dve, 1)

            norm_a(3)
            split_w2(0)
            mine.reset()

            xf = x_sb[:, :, :].rearrange("p n c -> p (n c)")

            def finish(t0):
                take(dve, back_s, 1)
                o = tmp.rearrange("p (i c) -> p i c", c=C)
                mine.inc(V.tensor_tensor(o, b2[:, 2, :].rearrange("p (i c) -> p i c", c=C), gate[:, 1:2, :].to_broadcast([P, TPC, C]), ALU.mult))
                mine.wait()
                V.tensor_tensor(xf[:, ds(t0, CW)], xf[:, ds(t0, CW)], tmp, ALU.add).then_inc(out_s, 1)
                mine.inc(V.memset(tick[:, 2:3], 0.0))
                mine.wait()

            def chunk(t_last, number):
                def add(e):
                    take(dve, cb_in[e], 16)
                    dve.wait_ge(y_ready, e + 1)
                    V.tensor_tensor(acc[:, :] if e == 0 else tmp, b2[:, e % 2, :], combB[e], ALU.mult).then_inc(y_free, 1)
                    mine.inc(V.memset(tick[:, 0:1], 0.0))
                    mine.wait()
                    if e == 0:
                        V.memset(tick[:, 3:4], 0.0).then_inc(cb_used, 1)
                    else:
                        V.tensor_tensor(acc[:, :], acc[:, :], tmp, ALU.add).then_inc(cb_used, 1)
                        mine.inc(V.memset(tick[:, 1:2], 0.0))
                        mine.wait()

                for e in range(E):
                    for f in range(FC):
                        n = e * FC + f
                        dve.wait_ge(hs_ready, n + 1)
                        V.tensor_tensor(hs_lo[:, e % 2, f, :], probs[:, e % 2, f, :], hs_hi[:, e % 2, f, :].bitcast(fp32), ALU.subtract).then_inc(lo_s, 1)
                    if e:
                        add(e - 1)
                    elif number != 0:
                        finish(t_last)
                    if number == 0:
                        if e == 0:
                            norm_b(3)
                            split_w2(1)
                        if e == 1:
                            residual(NC_ - 1)
                        if e == 3:
                            keep_logits(NC_ - 1)
                            route(1, 0)
                        if e == 5:
                            route(1, 1)
                    if number == 1 and e in (2, 6):
                        route(1, 2 + (e == 6))
                add(E - 1)
                V.memset(tick[:, 4:5], 0.0).then_inc(acc_s, 1)
                dve.sem_inc(y_ready, -E)
                dve.sem_inc(hs_ready, -E * FC)
                mine.reset()

            chunk(None, 0)
            chunk(0, 1)
            keep_weights(1)
            with dve.Fori(2, NC_) as c:
                chunk(dve.snap(c * CW - CW), None)
            finish((NC_ - 1) * CW)

        @block.scalar
        def _(act):
            for dst, src, done in ((ccol[:, :], a["ccol"], c_in), (wmod[:, :], a["wmod"], wmod_in)):
                act.dma_start(dst, src).then_inc(done, 16)
            act.wait_ge(c_in, 16)
            nc.scalar.activation(sil[:, :], ccol[:, :], ACT.Silu).then_inc(silu_c, 1)
            own = Own(act, act_s)

            def features(c, k):
                act.wait_ge(xT_ps, NC_ * k + c + 1)
                turned_ = b2[:, c % 2, :] if k == 0 else b1[:, 1, :] if c < NC_ - 1 else b2[:, 2, :]
                for dst in (hT, h_hi)[:1 if k == 0 or c < NC_ - 1 else 2]:
                    last = nc.scalar.activation(dst[:, c * CW:(c + 1) * CW], turned_, ACT.Identity,
                                                bias=modc[:, 2 * k:2 * k + 1], scale=modc[:, 2 * k + 1:2 * k + 2])
                last.then_inc(hT_s, 1)

            def scale_tokens(c):
                act.wait_ge(rstd_s, c + 1)
                for n in range(TPC * c, TPC * (c + 1)):
                    last = nc.scalar.activation(xn[:, n, :], x_sb[:, n, :], ACT.Identity, bias=nmr[:, n:n + 1], scale=rstd[:, n:n + 1])
                last.then_inc(xn_s, 1)

            scale_tokens(0)
            act.wait_ge(modc_s, 1)
            act.wait_ge(bqk_s, 1)
            features(0, 0)
            scale_tokens(1)
            for c in range(NC_):
                for n in range(2):
                    act.wait_ge(qk_ps, 2 * c + n + 1)
                    if c:
                        act.wait_ge(piece_s, 2 * (c - 1) + n + 1)
                    if c >= 2 and n == 0:
                        act.wait_ge(piece_out[c - 2], 6 * 16)
                    for dst in (q32[:, n, :], pieces[:, c % 2, n, 0, :]):
                        last = nc.scalar.activation(dst, b1[:, n, :], ACT.Identity, bias=bqk[:, n:n + 1], scale=D ** -0.5 if n == 0 else 1.0)
                    last.then_inc(q32_s, 1)
                if c + 1 < NC_:
                    features(c + 1, 0)
                for n in range(2):
                    act.wait_ge(res_s, 2 * c + n + 1)
                    nc.scalar.activation(pieces[:, c % 2, n, 1, :], res[:, n, :], ACT.Copy).then_inc(piece2_s, 1)
                if c + 2 < NC_:
                    scale_tokens(c + 2)

            def route_exp(k, b):
                n = slice(2 * TPC * k, 2 * TPC * (k + 1))
                if b == 0:
                    act.wait_ge(lg_s, k + 1)
                    nc.scalar.activation(pr[:, n, :], lg[:, n, :], ACT.Exp).then_inc(pe_s, 1)
                else:
                    act.wait_ge(d_s, k + 1)
                    nc.scalar.activation(wtop[:, 1, n], wtop[:, 0, n], ACT.Exp).then_inc(ed_s, 1)

            def group(first, last):
                n2 = 0

                def turned(u, n2):
                    act.wait_ge(s2_ready, n2)
                    copy = nc.scalar.activation(rows[:, u % 2, :], b2[0:3 * HG, (n2 - 1) % RING2, 0:CW // 2].bitcast(bf16), ACT.Copy)
                    if first and u == 0:
                        own.inc(copy)
                        own.wait()
                        send_rows(act, 0, 0)
                    else:
                        copy.then_inc(rows_s, 1)

                for u in turns(-1, first, last):
                    n2 += 1
                    turned(u, n2)
                for p in range(NSTEP + 1):
                    if p < NSTEP:
                        w = PASS2[p] // HG
                        if p >= 2:
                            act.wait_ge(pv_done, p - 1)
                        for hh in range(HG):
                            n2 += 1
                            act.wait_ge(s2_ready, n2)
                            nc.scalar.activation(probs[:, p % 2, hh, 0:w], b2[:, (n2 - 1) % RING2, 0:w], ACT.Exp).then_inc(exp_done, 1)
                        for u in turns(p, first, last):
                            n2 += 1
                            turned(u, n2)
                    if last and p in TURN:
                        features(TURN[p], 1)
                    if last and p in ROUTE_EXP:
                        route_exp(0, ROUTE_EXP[p])
                    if p in START[1:]:
                        j = START.index(p) - 1
                        act.wait_ge(pv_done, p)
                        nc.scalar.activation(yT[:, j % 2, :], pv[:, :], ACT.Copy).then_inc(yT_dve, 1)
                        nc.scalar.activation(tick[:, 8 + j:9 + j], ident[:, 0:1], ACT.Copy).then_inc(yT_pe, 1)
                act.sem_inc(s2_ready, -n2)
                act.sem_inc(pv_done, -NSTEP)

            group(True, False)
            with act.Fori(1, G - 1):
                group(False, False)
            group(False, True)

            def chunk(number):
                for n in range(E * FC):
                    e, f = divmod(n, FC)
                    if number == 0 and f == 0 and LAST_WAY.get(e) == "turn":
                        features(NC_ - 1, 1)
                    act.wait_ge(up_ready, n + 1)
                    for dst in (probs, hs_hi):
                        last = nc.scalar.activation(dst[:, e % 2, f, :], b1[:, n % RING1, :], ACT.Silu)
                    last.then_inc(hs_ready, 1)
                    if number in (0, 1) and n == 5 * FC - 1:
                        route_exp(1, number)
                act.sem_inc(up_ready, -E * FC)

            chunk(0)
            chunk(1)
            with act.Fori(2, NC_):
                chunk(None)

        @block.gpsimd
        def _(pool):
            own = Own(pool, pool_s)
            u32 = mybir.dt.uint32
            half = HG * T
            def clear_pads(k):
                pool.wait_ge(rstd_s, norms[0])
                own.wait()
                for aug in (q_aug, k_aug)[:k + 1]:
                    nc.gpsimd.memset(aug[PAD0:ROWS2, k * half:(k + 1) * half].bitcast(u32), 0).then_inc(pad_set[k], 1)
                pool.wait_ge(pad_set[k], k + 1)

            norms = [0]

            def deviation(c, setup=False):
                norms[0] += 1
                pool.wait_ge(var_s, norms[0])
                n = slice(TPC * c, TPC * (c + 1))
                own.inc(nc.gpsimd.tensor_scalar(rstd[:, n], mv[:, n, 1], EPS, None, ALU.add))
                own.wait()
                if setup:
                    own.inc(nc.gpsimd.tensor_tensor(rstd[:, n], rstd[:, n], neg_half[:, 0:TPC], ALU.pow))
                    own.wait()
                    own.inc(nc.gpsimd.tensor_tensor(nmr[:, n], rstd[:, n], mv[:, n, 0], ALU.mult))
                    own.wait()
                    nc.gpsimd.tensor_scalar(nmr[:, n], nmr[:, n], -1.0, None, ALU.mult).then_inc(rstd_s, 1)
                else:
                    nc.gpsimd.tensor_tensor(rstd[:, n], rstd[:, n], neg_half[:, 0:TPC], ALU.pow).then_inc(rstd_s, 1)

            own.inc(nc.gpsimd.memset(neg_half[:, :], -0.5))
            deviation(0, True)
            deviation(1, True)
            clear_pads(0)
            pool.wait_ge(w_in, 4 * 16)
            own.inc(nc.gpsimd.tensor_copy(identb[:, :], ident[:, :]))
            deviation(2, True)
            deviation(3, True)
            own.inc(nc.gpsimd.memset(v_cur[:, :, :, :], 0.0))
            own.wait()
            own.inc(nc.gpsimd.memset(v_cur[:, :, :, D:2 * D], 1.0))
            pool.wait_ge(v_s, NC_)
            clear_pads(1)
            pool.wait_ge(gate_s, 1)
            pool.wait_ge(mask_in, 3 * 16)
            nc.gpsimd.tensor_tensor(wproj[:, :, :], wproj[:, :, :], gate[:, 0:1, :].to_broadcast([P, G, C]), ALU.mult).then_inc(wp_s, 1)
            own.wait()

            def values(q, g):
                b = slice(TPC * q, TPC * (q + 1))
                src = v_all[:, b, ds(g * HG * D, HG * D)].rearrange("p b (h d) -> p b h d", d=D)
                nc.gpsimd.tensor_copy(v_cur[:, b, :, 0:D], src).then_inc(v_ready, 1)

            for q in range(3):
                values(q, 0)
            mine = Own(pool, pool_g)

            def cut_maxima(u):
                take(pool, nmax_s, 1)
                k = u % 2
                mine.inc(nc.gpsimd.tensor_copy(nmp[:, k, :, 0, :], nmax[:, k, :, :]))
                mine.wait()
                mine.inc(nc.gpsimd.tensor_tensor(nres[:, k, :, :], nmax[:, k, :, :], nmp[:, k, :, 0, :], ALU.subtract))
                mine.wait()
                mine.inc(nc.gpsimd.tensor_copy(nmp[:, k, :, 1, :], nres[:, k, :, :]))
                mine.wait()
                nc.gpsimd.tensor_tensor(nmp[:, k, :, 2, :], nres[:, k, :, :], nmp[:, k, :, 1, :], ALU.subtract).then_inc(nmp_s, 1)

            def spread(j):
                take(pool, rl_s, 1)
                k = j % 2
                nc.gpsimd.tensor_copy(yN[:, k, :, :], rl[:, k, :].unsqueeze(2).to_broadcast([P, CW // 32, 32])).then_inc(rB_s, 1)

            def normal(j, g):
                take(pool, rT_s, 1)
                k = j % 2
                nc.gpsimd.tensor_tensor(yn[:, ds(g * T + j * CW, CW)], yT[:, k, :], yB[:, k, :, :].rearrange("p b q -> p (b q)"),
                                        ALU.mult).then_inc(yn_s, 1)

            def group(g, first, last):
                for p in range(-1, NSTEP + 1):
                    for u in turns(p, first, last):
                        cut_maxima(u)
                    if p == 1:
                        take(pool, v_used, 1)
                        values(3, g)
                    if last and p in PROJECT:
                        deviation(PROJECT[p])
                    for base, j in NORM_AT:
                        if not (first and j == 3):
                            if p == base + 1:
                                spread(j)
                            if p == base + 3:
                                normal(j, g - 1 if j == 3 else g)
                    for q in range(3):
                        if p == START[3] + TPC * (q + 1) + 1:
                            take(pool, v_used, 1)
                            if not last:
                                values(q, g + 1)
                    if last and p in HIGH:
                        c = HIGH[p]
                        pool.wait_ge(hT_s, NC_ + c + 1)
                        t = slice(CW * c, CW * (c + 1))
                        nc.gpsimd.tensor_copy(h_hi[:, t], hT[:, t]).then_inc(hhi_s, 1)
                    if last and p in W1_AT:
                        e = W1_AT.index(p)
                        if e == 0:
                            pool.wait_ge(late_in, 5 * 16)
                        w = slice(e * F, (e + 1) * F)
                        own.inc(nc.gpsimd.tensor_copy(w1_hi[:, w], w1T[:, w]))
                        own.wait()
                        nc.gpsimd.tensor_tensor(w1_lo[:, w], w1T[:, w], w1_hi[:, w].bitcast(fp32), ALU.subtract).then_inc(w1_s, 1)
                mine.reset()

            group(0, True, False)
            with pool.Fori(1, G - 1) as g:
                group(g, False, False)
            group(G - 1, False, True)
            spread(3)
            normal(3, G - 1)
            for e in range(2, E):
                n = slice(e * FC, (e + 1) * FC)
                own.inc(nc.gpsimd.tensor_copy(w2_hi[:, n, :], w2T[:, n, :]))
                own.wait()
                nc.gpsimd.tensor_tensor(w2_lo[:, n, :], w2T[:, n, :], w2_hi[:, n, :].bitcast(fp32), ALU.subtract).then_inc(w2_pool, 1)
                if e == 3:
                    deviation(NC_ - 1)


def kernel(L0_attn_x, L0_attn_W_attn, L0_attn_b_attn, L0_attn_W_proj, L0_attn_b_proj, L0_ffn_router_w, L0_ffn_w1, L0_ffn_w2,
           L0_ffn_expert_scale, L0_c, L0_wmod):
    import ml_dtypes
    import concourse.bacc as bacc
    from concourse.bass_utils import run_bass_kernel_spmd

    f32 = np.float32
    cont = np.ascontiguousarray
    wproj = np.zeros((HG, 32, G, C), f32)
    wproj[:, 0:D] = np.asarray(L0_attn_W_proj).reshape(G, HG, D, C).transpose(1, 2, 0, 3)
    wproj[0, D, 0] = np.asarray(L0_attn_b_proj)
    slope = (2.0 ** -np.arange(1, H + 1)).astype(f32)[:, None]
    t = np.arange(T)
    one = np.ones((H, T), f32)
    alibi = np.stack([np.stack([-P * slope * (t // P), one, -slope * (t % P), one]),
                      np.stack([one, P * slope * (t // P), one, slope * (t % P)])]).astype(ml_dtypes.bfloat16)
    q, k = np.arange(P)[:, None], np.arange(P)[None, :]
    mask = np.zeros((P, CW), f32)
    mask[:, CW - P:] = np.where(k > q, BIG, 0.0)
    ee = np.arange(E)
    arrays = {
        "x": cont(np.asarray(L0_attn_x).reshape(T, C)),
        "wqkv": cont(L0_attn_W_attn),
        "bqk": cont(np.asarray(L0_attn_b_attn)[:2 * C].reshape(2, C).T),
        "bv": cont(np.asarray(L0_attn_b_attn)[2 * C:].reshape(1, C)),
        "wproj": wproj.reshape(P, G, C),
        "rwT": cont(np.asarray(L0_ffn_router_w).T),
        "w1T": cont(np.asarray(L0_ffn_w1).transpose(2, 0, 1).reshape(C, E * F)),
        "w2T": cont(np.asarray(L0_ffn_w2).reshape(E, C, FC, P).transpose(3, 0, 2, 1).reshape(P, E * FC, C)),
        "scale": cont(np.asarray(L0_ffn_expert_scale).reshape(1, E)),
        "ccol": cont(np.asarray(L0_c).reshape(C, 1)),
        "wmod": cont(L0_wmod),
        "ident": np.eye(P, dtype=f32),
        "mask": mask,
        "maskT": cont(mask[:, CW - P:].T).astype(ml_dtypes.bfloat16),
        "alibi": alibi,
        "ones3": np.ones((3, HG, T), ml_dtypes.bfloat16),
        "tri8": cont(np.broadcast_to((ee[None, :] < ee[:, None]).astype(f32), (P, E, E))),
    }
    nc = bacc.Bacc("TRN2", target_bir_lowering=False, num_devices=1)
    aps = {n: nc.dram_tensor(f"in_{n}", v.shape, mybir.dt.from_np(v.dtype), kind="ExternalInput").ap() for n, v in arrays.items()}
    aps["out"] = nc.dram_tensor("out_0", (T, C), mybir.dt.float32, kind="ExternalOutput").ap()
    build(nc, aps)
    r = run_bass_kernel_spmd(nc, [{f"in_{n}": v for n, v in arrays.items()}], core_ids=[0])
    return np.asarray(r.results[0]["out_0"]).reshape(1, T, C)
```
